# Optimizing a Trainium2 kernel written in Bass

```python
import numpy as np
import jax
import jax.numpy as jnp

def _softmax(x, axis=-1):
    return jax.nn.softmax(x, axis=axis)

def _gelu(x):
    return jax.nn.gelu(x, approximate=True)

def _silu(x):
    return jax.nn.silu(x)

def _sigmoid(x):
    return jax.nn.sigmoid(x)

def _layernorm(x, axis=-1, eps=1e-05):
    m = jnp.mean(x, axis=axis, keepdims=True)
    v = jnp.var(x, axis=axis, keepdims=True)
    return (x - m) / jnp.sqrt(v + eps)

def _scatter_add(tgt, idx, src, axis=0):
    return tgt.at[idx].add(src)

def _segment_sum(src, seg, n):
    return jax.ops.segment_sum(src, seg, n)
kernel_name = 'mk_xattn_ffn_d4_seqx_r8_594575'

def setup_inputs(seed: int=0):
    np.random.seed(seed)
    _w = jnp.asarray

    def _rec_inputs():
        import jax
        import jax.numpy as jnp
        _rk = jax.random.key(seed)
        x = -0.0002928 + 1 * jax.random.normal(jax.random.fold_in(_rk, 1), (16, 64, 512), jnp.float32)
        _lenS = 64 - jax.random.randint(jax.random.fold_in(_rk, 7), (16,), 0, max(1, 64 // 4) + 1, jnp.int32)
        _lenS2 = 64 - jax.random.randint(jax.random.fold_in(_rk, 8), (16,), 0, max(1, 64 // 4) + 1, jnp.int32)
        _ctx_4096P = jax.random.normal(jax.random.fold_in(_rk, 11), (16, 16, 512), jnp.float32)
        _ctx_4096c = jax.random.dirichlet(jax.random.fold_in(_rk, 511), 0.3 * jnp.ones((16,), jnp.float32), (16, 64))
        _ctx_4096t = jnp.einsum('bsk,bkd->bsd', _ctx_4096c, _ctx_4096P)
        _ctx_4096t = _ctx_4096t * jax.lax.rsqrt(jnp.mean(jnp.square(_ctx_4096t)) + 1e-12) * 0.953939
        ctx_4096 = -2.8382e-05 + 0.999851 * (_ctx_4096t + 0.3 * jax.random.normal(jax.random.fold_in(_rk, 611), (16, 64, 512), jnp.float32))
        fside_Bx32xSxS2_0 = 0.000150688 + 1.00006 * jax.random.normal(jax.random.fold_in(_rk, 14), (16, 32, 64, 64), jnp.float32)
        _validS = jnp.arange(64)[None, :] < _lenS[:, None]
        _validS2 = jnp.arange(64)[None, :] < _lenS2[:, None]
        _causal = jnp.tril(jnp.ones((64, 64), dtype=bool))
        mask_1x1xSxS2_ff0 = jnp.where(jnp.ones((1, 1, 64, 64), dtype=bool), 0.0, -1000000000.0).astype(jnp.float32)
        mask_BxSxS2_bk0 = jnp.logical_not(jnp.broadcast_to(_validS2[:, None, :], (16, 64, 64)))
        return (x, ctx_4096, fside_Bx32xSxS2_0, mask_1x1xSxS2_ff0, mask_BxSxS2_bk0)
    x, ctx_4096, fside_Bx32xSxS2_0, mask_1x1xSxS2_ff0, mask_BxSxS2_bk0 = _rec_inputs()

    def _L0_xattn_setup():
        import jax, jax.numpy as jnp
        import numpy as np
        NUM_HEADS = 32
        NUM_KV_HEADS = 8
        HEAD_DIM = 128
        HIDDEN = 512
        EPS = 1e-05

        def rmsnorm(x, w, eps=EPS):
            xf = x.astype(jnp.float32)
            var = jnp.mean(xf * xf, axis=-1, keepdims=True)
            return w * (xf * jax.lax.rsqrt(var + eps)).astype(x.dtype)
        key = jax.random.key(seed)
        ks = jax.random.split(key, 10)
        B, Q, KV = (1, 128, 6404)
        s = 1.0 / np.sqrt(HIDDEN)
        return {'hidden_states': jax.random.normal(ks[0], (B, Q, HIDDEN), jnp.float32), 'cross_attention_states': jax.random.normal(ks[1], (B, KV, HIDDEN), jnp.float32), 'attention_mask': jnp.zeros((B, 1, Q, KV), jnp.float32), 'q_proj_w': jax.random.normal(ks[2], (NUM_HEADS * HEAD_DIM, HIDDEN), jnp.float32) * s, 'k_proj_w': jax.random.normal(ks[3], (NUM_KV_HEADS * HEAD_DIM, HIDDEN), jnp.float32) * s, 'v_proj_w': jax.random.normal(ks[4], (NUM_KV_HEADS * HEAD_DIM, HIDDEN), jnp.float32) * s, 'o_proj_w': jax.random.normal(ks[5], (HIDDEN, NUM_HEADS * HEAD_DIM), jnp.float32) * s, 'q_norm_w': jnp.ones((HEAD_DIM,), jnp.float32), 'k_norm_w': jnp.ones((HEAD_DIM,), jnp.float32)}
    _L0_xattn_all = _L0_xattn_setup()
    _L0_xattn_in = {k: v for k, v in _L0_xattn_all.items() if k in ('q_proj_w', 'k_proj_w', 'v_proj_w', 'o_proj_w', 'q_norm_w', 'k_norm_w')}
    del _L0_xattn_all

    def _L0_ffn_setup():
        import jax, jax.numpy as jnp
        import numpy as np

        @jax.custom_vjp
        def ste_sign(w):
            return jnp.sign(w)

        def _ste_fwd(w):
            return (jnp.sign(w), w)

        def _ste_bwd(w, g):
            mask = ((w > -1) & (w < 1)).astype(g.dtype)
            return (g * mask,)
        ste_sign.defvjp(_ste_fwd, _ste_bwd)
        key = jax.random.key(seed)
        k = jax.random.split(key, 6)
        B, S, H, O, E = (4, 256, 512, 512, 8)
        return {'x': jax.random.normal(k[0], (B, S, H), dtype=jnp.float32), 'weight': jax.random.normal(k[1], (O, H), dtype=jnp.float32) * 0.02, 'bias': jax.random.normal(k[2], (O,), dtype=jnp.float32) * 0.02, 'gate_w': jax.random.normal(k[3], (E, H), dtype=jnp.float32) * 0.02, 'in_channel_scale': jax.random.normal(k[4], (E, H), dtype=jnp.float32), 'out_channel_scale': jax.random.normal(k[5], (E, O), dtype=jnp.float32)}
    _L0_ffn_all = _L0_ffn_setup()
    _L0_ffn_in = {k: v for k, v in _L0_ffn_all.items() if k in ('weight', 'bias', 'gate_w', 'in_channel_scale', 'out_channel_scale')}
    del _L0_ffn_all

    def _L1_xattn_setup():
        import jax, jax.numpy as jnp
        import numpy as np
        TEXT_DIM = 512
        FEATURE_DIM = 512

        def _xavier_uniform(key, shape):
            fan_in, fan_out = (shape[1], shape[0])
            limit = float(np.sqrt(6.0 / (fan_in + fan_out)))
            return jax.random.uniform(key, shape, jnp.float32, -limit, limit)
        key = jax.random.key(seed)
        k1, k2, k3, k4 = jax.random.split(key, 4)
        text = jax.random.normal(k1, (8, 256, TEXT_DIM), jnp.float32)
        features = jax.random.normal(k2, (8, 72, FEATURE_DIM), jnp.float32)
        Wq = _xavier_uniform(k3, (FEATURE_DIM, TEXT_DIM))
        bq = jnp.zeros((FEATURE_DIM,), jnp.float32)
        Wk = _xavier_uniform(k4, (FEATURE_DIM, FEATURE_DIM))
        bk = jnp.zeros((FEATURE_DIM,), jnp.float32)
        return {'text': text, 'features': features, 'Wq': Wq, 'bq': bq, 'Wk': Wk, 'bk': bk}
    _L1_xattn_all = _L1_xattn_setup()
    _L1_xattn_in = {k: v for k, v in _L1_xattn_all.items() if k in ('Wq', 'bq', 'Wk', 'bk')}
    del _L1_xattn_all

    def _L1_ffn_setup():
        import math
        import jax, jax.numpy as jnp
        import numpy as np
        SCALING = 16.0 / 32.0

        def real_fourier_orthogonal_multiply(c):
            n = c.shape[-1]
            sqrt_n = math.sqrt(n)
            pair_scale = math.sqrt(n / 2.0)
            max_f = (n - 1) // 2
            work = c.astype(jnp.float32)
            dc = (work[..., 0] * sqrt_n)[..., None].astype(jnp.complex64)
            cos = work[..., 1:1 + 2 * max_f:2] * pair_scale
            sin = work[..., 2:2 + 2 * max_f:2] * pair_scale
            mid = (cos - 1j * sin).astype(jnp.complex64)
            parts = [dc, mid]
            if n % 2 == 0:
                parts.append((work[..., -1] * sqrt_n)[..., None].astype(jnp.complex64))
            spectrum = jnp.concatenate(parts, axis=-1)
            return jnp.fft.irfft(spectrum, n=n, axis=-1).astype(c.dtype)
        key = jax.random.key(seed)
        ks = jax.random.split(key, 9)
        B, S, D_in, D_out, R0, R1, E = (4, 256, 512, 512, 32, 8, 3)
        x = jax.random.normal(ks[0], (B, S, D_in), dtype=jnp.float32)
        W_base = jax.random.normal(ks[1], (D_out, D_in), dtype=jnp.float32) * 0.02
        b_base = jax.random.normal(ks[2], (D_out,), dtype=jnp.float32) * 0.02
        enc0 = jax.random.normal(ks[3], (R0, D_in), dtype=jnp.float32) * 0.02
        enc1 = jax.random.normal(ks[4], (R1, D_in), dtype=jnp.float32) * 0.02
        coefs0 = jax.random.normal(ks[5], (E, D_out, R0), dtype=jnp.float32) * 0.02
        coefs1 = jax.random.normal(ks[6], (E, D_out, R1), dtype=jnp.float32) * 0.02
        mask0 = jax.random.randint(ks[7], (E, D_out, R0), 0, 2).astype(bool)
        mask1 = jax.random.randint(ks[8], (E, D_out, R1), 0, 2).astype(bool)
        return dict(x=x, W_base=W_base, b_base=b_base, enc0=enc0, enc1=enc1, coefs0=coefs0, coefs1=coefs1, mask0=mask0, mask1=mask1)
    _L1_ffn_all = _L1_ffn_setup()
    _L1_ffn_in = {k: v for k, v in _L1_ffn_all.items() if k in ('W_base', 'b_base', 'enc0', 'enc1', 'coefs0', 'coefs1', 'mask0', 'mask1')}
    del _L1_ffn_all

    def _L2_xattn_setup():
        import math
        import jax, jax.numpy as jnp
        import numpy as np
        B, S, D = (2, 128, 512)
        H, DH = (32, 128)
        key = jax.random.key(seed)
        ks = jax.random.split(key, 8)
        scale = 1.0 / math.sqrt(D)
        return {'hidden_q': jax.random.normal(ks[0], (B, S, D), jnp.float32), 'hidden_kv': jax.random.normal(ks[1], (B, S, D), jnp.float32), 'attention_mask': jax.random.randint(ks[2], (B, S, S), 0, 2) > 0, 'position_bias': jax.random.normal(ks[3], (B, H, S, S), jnp.float32), 'Wq': jax.random.normal(ks[4], (D, H * DH), jnp.float32) * scale, 'Wk': jax.random.normal(ks[5], (D, H * DH), jnp.float32) * scale, 'Wv': jax.random.normal(ks[6], (D, H * DH), jnp.float32) * scale, 'Wo': jax.random.normal(ks[7], (H * DH, D), jnp.float32) * scale}
    _L2_xattn_all = _L2_xattn_setup()
    _L2_xattn_in = {k: v for k, v in _L2_xattn_all.items() if k in ('Wq', 'Wk', 'Wv', 'Wo')}
    del _L2_xattn_all

    def _L2_ffn_setup():
        import jax, jax.numpy as jnp
        import numpy as np
        B, S, D, O, E, R = (4, 256, 512, 512, 8, 16)
        SCALING = 32.0 / 16.0
        MAX_THRESHOLD = 0.125
        key = jax.random.key(seed)
        ks = jax.random.split(key, 8)
        return {'x': jax.random.normal(ks[0], (B, S, D), jnp.float32), 'W_base': jax.random.normal(ks[1], (O, D), jnp.float32) * (1.0 / np.sqrt(D)), 'b_base': jax.random.normal(ks[2], (O,), jnp.float32) * 0.02, 'W_gate': jax.random.normal(ks[3], (E, D), jnp.float32) * (1.0 / np.sqrt(D)), 'W_thr': jax.random.normal(ks[4], (D,), jnp.float32) * (1.0 / np.sqrt(D)), 'b_thr': jax.random.normal(ks[5], (1,), jnp.float32) * 0.02, 'A_w': jax.random.normal(ks[6], (E, R, D), jnp.float32) * (1.0 / np.sqrt(D)), 'B_w': jax.random.normal(ks[7], (E, O, R), jnp.float32) * (1.0 / np.sqrt(R))}
    _L2_ffn_all = _L2_ffn_setup()
    _L2_ffn_in = {k: v for k, v in _L2_ffn_all.items() if k in ('W_base', 'b_base', 'W_gate', 'W_thr', 'b_thr', 'A_w', 'B_w')}
    del _L2_ffn_all

    def _L3_xattn_setup():
        import jax, jax.numpy as jnp
        import numpy as np
        import math
        HIDDEN = 512
        N_HEADS = 32
        HEAD_DIM = 128
        N_KV_HEADS = 4
        N_GROUPS = N_HEADS // N_KV_HEADS
        key = jax.random.key(seed)
        ks = jax.random.split(key, 6)
        B, NL, S = (8, 64, 512)
        latents = jax.random.normal(ks[0], (B, NL, HIDDEN), dtype=jnp.float32)
        context = jax.random.normal(ks[1], (B, S, HIDDEN), dtype=jnp.float32)
        scale = 1.0 / math.sqrt(HIDDEN)
        Wq = jax.random.normal(ks[2], (HIDDEN, N_HEADS * HEAD_DIM), dtype=jnp.float32) * scale
        Wk = jax.random.normal(ks[3], (HIDDEN, N_KV_HEADS * HEAD_DIM), dtype=jnp.float32) * scale
        Wv = jax.random.normal(ks[4], (HIDDEN, N_KV_HEADS * HEAD_DIM), dtype=jnp.float32) * scale
        Wo = jax.random.normal(ks[5], (N_HEADS * HEAD_DIM, HIDDEN), dtype=jnp.float32) * scale
        return {'latents': latents, 'context': context, 'Wq': Wq, 'Wk': Wk, 'Wv': Wv, 'Wo': Wo}
    _L3_xattn_all = _L3_xattn_setup()
    _L3_xattn_in = {k: v for k, v in _L3_xattn_all.items() if k in ('Wq', 'Wk', 'Wv', 'Wo')}
    del _L3_xattn_all

    def _L3_ffn_setup():
        import jax, jax.numpy as jnp
        import numpy as np
        NUM_EXPERTS = 8
        TOP_K = 2
        RANK = 16
        LORA_ALPHA = 32
        SCALING = LORA_ALPHA / RANK
        key = jax.random.key(seed)
        ks = jax.random.split(key, 6)
        B, S, D_IN, D_OUT = (4, 256, 512, 512)
        x = jax.random.normal(ks[0], (B, S, D_IN), dtype=jnp.float32)
        W_base = jax.random.normal(ks[1], (D_OUT, D_IN), dtype=jnp.float32) * 0.02
        b_base = jax.random.normal(ks[2], (D_OUT,), dtype=jnp.float32) * 0.02
        W_router = jax.random.normal(ks[3], (NUM_EXPERTS, D_IN), dtype=jnp.float32) * 0.02
        A = jax.random.normal(ks[4], (NUM_EXPERTS, RANK, D_IN), dtype=jnp.float32) * 0.02
        Bm = jax.random.normal(ks[5], (D_OUT, RANK), dtype=jnp.float32) * 0.02
        Bm = jnp.broadcast_to(Bm, (NUM_EXPERTS, D_OUT, RANK)) * jnp.arange(1, NUM_EXPERTS + 1, dtype=jnp.float32)[:, None, None] * 0.2
        return {'x': x, 'W_base': W_base, 'b_base': b_base, 'W_router': W_router, 'A': A, 'B': Bm}
    _L3_ffn_all = _L3_ffn_setup()
    _L3_ffn_in = {k: v for k, v in _L3_ffn_all.items() if k in ('W_base', 'b_base', 'W_router', 'A', 'B')}
    del _L3_ffn_all
    return {'x': x, 'ctx_4096': ctx_4096, 'fside_Bx32xSxS2_0': fside_Bx32xSxS2_0, 'mask_1x1xSxS2_ff0': mask_1x1xSxS2_ff0, 'mask_BxSxS2_bk0': mask_BxSxS2_bk0, 'L0_xattn_q_proj_w': _L0_xattn_in['q_proj_w'], 'L0_xattn_k_proj_w': _L0_xattn_in['k_proj_w'], 'L0_xattn_v_proj_w': _L0_xattn_in['v_proj_w'], 'L0_xattn_o_proj_w': _L0_xattn_in['o_proj_w'], 'L0_xattn_q_norm_w': _L0_xattn_in['q_norm_w'], 'L0_xattn_k_norm_w': _L0_xattn_in['k_norm_w'], 'L0_ffn_weight': _L0_ffn_in['weight'], 'L0_ffn_bias': _L0_ffn_in['bias'], 'L0_ffn_gate_w': _L0_ffn_in['gate_w'], 'L0_ffn_in_channel_scale': _L0_ffn_in['in_channel_scale'], 'L0_ffn_out_channel_scale': _L0_ffn_in['out_channel_scale'], 'L1_xattn_Wq': _L1_xattn_in['Wq'], 'L1_xattn_bq': _L1_xattn_in['bq'], 'L1_xattn_Wk': _L1_xattn_in['Wk'], 'L1_xattn_bk': _L1_xattn_in['bk'], 'L1_ffn_W_base': _L1_ffn_in['W_base'], 'L1_ffn_b_base': _L1_ffn_in['b_base'], 'L1_ffn_enc0': _L1_ffn_in['enc0'], 'L1_ffn_enc1': _L1_ffn_in['enc1'], 'L1_ffn_coefs0': _L1_ffn_in['coefs0'], 'L1_ffn_coefs1': _L1_ffn_in['coefs1'], 'L1_ffn_mask0': _L1_ffn_in['mask0'], 'L1_ffn_mask1': _L1_ffn_in['mask1'], 'L2_xattn_Wq': _L2_xattn_in['Wq'], 'L2_xattn_Wk': _L2_xattn_in['Wk'], 'L2_xattn_Wv': _L2_xattn_in['Wv'], 'L2_xattn_Wo': _L2_xattn_in['Wo'], 'L2_ffn_W_base': _L2_ffn_in['W_base'], 'L2_ffn_b_base': _L2_ffn_in['b_base'], 'L2_ffn_W_gate': _L2_ffn_in['W_gate'], 'L2_ffn_W_thr': _L2_ffn_in['W_thr'], 'L2_ffn_b_thr': _L2_ffn_in['b_thr'], 'L2_ffn_A_w': _L2_ffn_in['A_w'], 'L2_ffn_B_w': _L2_ffn_in['B_w'], 'L3_xattn_Wq': _L3_xattn_in['Wq'], 'L3_xattn_Wk': _L3_xattn_in['Wk'], 'L3_xattn_Wv': _L3_xattn_in['Wv'], 'L3_xattn_Wo': _L3_xattn_in['Wo'], 'L3_ffn_W_base': _L3_ffn_in['W_base'], 'L3_ffn_b_base': _L3_ffn_in['b_base'], 'L3_ffn_W_router': _L3_ffn_in['W_router'], 'L3_ffn_A': _L3_ffn_in['A'], 'L3_ffn_B': _L3_ffn_in['B']}

def reference(x, ctx_4096, fside_Bx32xSxS2_0, mask_1x1xSxS2_ff0, mask_BxSxS2_bk0, L0_xattn_q_proj_w, L0_xattn_k_proj_w, L0_xattn_v_proj_w, L0_xattn_o_proj_w, L0_xattn_q_norm_w, L0_xattn_k_norm_w, L0_ffn_weight, L0_ffn_bias, L0_ffn_gate_w, L0_ffn_in_channel_scale, L0_ffn_out_channel_scale, L1_xattn_Wq, L1_xattn_bq, L1_xattn_Wk, L1_xattn_bk, L1_ffn_W_base, L1_ffn_b_base, L1_ffn_enc0, L1_ffn_enc1, L1_ffn_coefs0, L1_ffn_coefs1, L1_ffn_mask0, L1_ffn_mask1, L2_xattn_Wq, L2_xattn_Wk, L2_xattn_Wv, L2_xattn_Wo, L2_ffn_W_base, L2_ffn_b_base, L2_ffn_W_gate, L2_ffn_W_thr, L2_ffn_b_thr, L2_ffn_A_w, L2_ffn_B_w, L3_xattn_Wq, L3_xattn_Wk, L3_xattn_Wv, L3_xattn_Wo, L3_ffn_W_base, L3_ffn_b_base, L3_ffn_W_router, L3_ffn_A, L3_ffn_B):
    import jax
    import jax.numpy as jnp

    def _L0_xattn_ref(hidden_states, cross_attention_states, attention_mask, q_proj_w, k_proj_w, v_proj_w, o_proj_w, q_norm_w, k_norm_w):
        import jax, jax.numpy as jnp
        import numpy as np
        NUM_HEADS = 32
        NUM_KV_HEADS = 8
        HEAD_DIM = 128
        HIDDEN = 512
        EPS = 1e-05

        def rmsnorm(x, w, eps=EPS):
            xf = x.astype(jnp.float32)
            var = jnp.mean(xf * xf, axis=-1, keepdims=True)
            return w * (xf * jax.lax.rsqrt(var + eps)).astype(x.dtype)
        B, Q, _ = hidden_states.shape
        KV = cross_attention_states.shape[1]
        n_rep = NUM_HEADS // NUM_KV_HEADS
        q = (hidden_states @ q_proj_w.T).reshape(B, Q, NUM_HEADS, HEAD_DIM).transpose(0, 2, 1, 3)
        k = (cross_attention_states @ k_proj_w.T).reshape(B, KV, NUM_KV_HEADS, HEAD_DIM).transpose(0, 2, 1, 3)
        v = (cross_attention_states @ v_proj_w.T).reshape(B, KV, NUM_KV_HEADS, HEAD_DIM).transpose(0, 2, 1, 3)
        q = rmsnorm(q, q_norm_w)
        k = jnp.repeat(k, n_rep, axis=1)
        v = jnp.repeat(v, n_rep, axis=1)
        k = rmsnorm(k, k_norm_w)
        scale = 1.0 / np.sqrt(HEAD_DIM)
        scores = jnp.einsum('bhqd,bhkd->bhqk', q, k) * scale + attention_mask
        attn = jax.nn.softmax(scores.astype(jnp.float32), axis=-1).astype(q.dtype)
        out = jnp.einsum('bhqk,bhkd->bhqd', attn, v)
        out = out.transpose(0, 2, 1, 3).reshape(B, Q, NUM_HEADS * HEAD_DIM)
        return out @ o_proj_w.T

    def _L0_ffn_ref(x, weight, bias, gate_w, in_channel_scale, out_channel_scale):
        import jax, jax.numpy as jnp
        import numpy as np

        @jax.custom_vjp
        def ste_sign(w):
            return jnp.sign(w)

        def _ste_fwd(w):
            return (jnp.sign(w), w)

        def _ste_bwd(w, g):
            mask = ((w > -1) & (w < 1)).astype(g.dtype)
            return (g * mask,)
        ste_sign.defvjp(_ste_fwd, _ste_bwd)
        B, S, H = x.shape
        xf = x.reshape(-1, H)
        router_logits = xf @ gate_w.T
        routing = jax.nn.softmax(router_logits.astype(jnp.float32), axis=1).astype(x.dtype)
        in_scale = routing @ in_channel_scale
        out_scale = routing @ out_channel_scale
        wb = ste_sign(weight)
        out = xf * in_scale @ wb.T * out_scale + bias
        return out.reshape(B, S, -1)

    def _L1_xattn_ref(text, features, Wq, bq, Wk, bk):
        import jax, jax.numpy as jnp
        import numpy as np
        TEXT_DIM = 512
        FEATURE_DIM = 512

        def _xavier_uniform(key, shape):
            fan_in, fan_out = (shape[1], shape[0])
            limit = float(np.sqrt(6.0 / (fan_in + fan_out)))
            return jax.random.uniform(key, shape, jnp.float32, -limit, limit)
        Q = jnp.einsum('btx,dx->btd', text, Wq) + bq
        K = jnp.einsum('bpx,dx->bpd', features, Wk) + bk
        scale = 1.0 / jnp.sqrt(jnp.asarray(K.shape[-1], K.dtype))
        scores = jnp.einsum('btd,bpd->btp', Q, K) * scale
        attn = jax.nn.softmax(scores, axis=-1)
        attended = jnp.einsum('btp,bpd->btd', attn, features)
        return attended

    def _L1_ffn_ref(x, W_base, b_base, enc0, enc1, coefs0, coefs1, mask0, mask1):
        import math
        import jax, jax.numpy as jnp
        import numpy as np
        SCALING = 16.0 / 32.0

        def real_fourier_orthogonal_multiply(c):
            n = c.shape[-1]
            sqrt_n = math.sqrt(n)
            pair_scale = math.sqrt(n / 2.0)
            max_f = (n - 1) // 2
            work = c.astype(jnp.float32)
            dc = (work[..., 0] * sqrt_n)[..., None].astype(jnp.complex64)
            cos = work[..., 1:1 + 2 * max_f:2] * pair_scale
            sin = work[..., 2:2 + 2 * max_f:2] * pair_scale
            mid = (cos - 1j * sin).astype(jnp.complex64)
            parts = [dc, mid]
            if n % 2 == 0:
                parts.append((work[..., -1] * sqrt_n)[..., None].astype(jnp.complex64))
            spectrum = jnp.concatenate(parts, axis=-1)
            return jnp.fft.irfft(spectrum, n=n, axis=-1).astype(c.dtype)
        base = jnp.einsum('bsd,od->bso', x, W_base) + b_base
        e0 = jnp.einsum('bsd,rd->bsr', x, enc0)
        e1 = jnp.einsum('bsd,rd->bsr', x, enc1)
        w0 = coefs0 * mask0.astype(coefs0.dtype)
        w1 = coefs1 * mask1.astype(coefs1.dtype)
        decoded = jnp.einsum('bsr,eor->ebso', e0, w0) + jnp.einsum('bsr,eor->ebso', e1, w1)
        transformed = real_fourier_orthogonal_multiply(decoded)
        update = transformed.sum(axis=0)
        return base + update * SCALING

    def _L2_xattn_ref(hidden_q, hidden_kv, attention_mask, position_bias, Wq, Wk, Wv, Wo):
        import math
        import jax, jax.numpy as jnp
        import numpy as np
        B, S, D = (2, 128, 512)
        H, DH = (32, 128)
        b, len_q, _ = hidden_q.shape
        len_k = hidden_kv.shape[1]
        q = (hidden_q @ Wq).reshape(b, len_q, H, DH).transpose(0, 2, 1, 3)
        k = (hidden_kv @ Wk).reshape(b, len_k, H, DH).transpose(0, 2, 1, 3)
        v = (hidden_kv @ Wv).reshape(b, len_k, H, DH).transpose(0, 2, 1, 3)
        score = jnp.einsum('bhqd,bhkd->bhqk', q, k) / math.sqrt(DH)
        score = score + position_bias
        mask = attention_mask[:, None, :, :]
        score = jnp.where(mask, score, -jnp.inf)
        probs = jax.nn.softmax(score, axis=-1)
        probs = jnp.where(mask, probs, 0.0)
        ctx = jnp.einsum('bhqk,bhkd->bhqd', probs, v)
        ctx = ctx.transpose(0, 2, 1, 3).reshape(b, len_q, H * DH)
        out = ctx @ Wo
        return out

    def _L2_ffn_ref(x, W_base, b_base, W_gate, W_thr, b_thr, A_w, B_w):
        import jax, jax.numpy as jnp
        import numpy as np
        B, S, D, O, E, R = (4, 256, 512, 512, 8, 16)
        SCALING = 32.0 / 16.0
        MAX_THRESHOLD = 0.125
        base = jnp.einsum('bsd,od->bso', x, W_base) + b_base
        xf = x.reshape(-1, D)
        gate = jax.nn.softmax(xf @ W_gate.T, axis=-1)
        thr = jax.nn.sigmoid(xf @ W_thr + b_thr[0]) * MAX_THRESHOLD
        adapted = gate - thr[:, None]
        selected = (adapted >= 0).astype(x.dtype)
        w = adapted * selected
        wsum = jnp.sum(w, axis=-1, keepdims=True)
        wsum = jnp.where(wsum == 0, jnp.ones_like(wsum), wsum)
        w = w / wsum
        h = jnp.einsum('nd,erd->ner', xf, A_w)
        moe = jnp.einsum('ner,ne,eor->no', h, w, B_w) * SCALING
        return base + moe.reshape(base.shape)

    def _L3_xattn_ref(latents, context, Wq, Wk, Wv, Wo):
        import jax, jax.numpy as jnp
        import numpy as np
        import math
        HIDDEN = 512
        N_HEADS = 32
        HEAD_DIM = 128
        N_KV_HEADS = 4
        N_GROUPS = N_HEADS // N_KV_HEADS
        b, q_len, _ = latents.shape
        kv_len = q_len + context.shape[1]
        hidden_states = jnp.concatenate([context, latents], axis=1)
        q = (latents @ Wq).reshape(b, q_len, N_KV_HEADS, N_GROUPS, HEAD_DIM)
        k = (hidden_states @ Wk).reshape(b, kv_len, N_KV_HEADS, HEAD_DIM)
        v = (hidden_states @ Wv).reshape(b, kv_len, N_KV_HEADS, HEAD_DIM)
        scale = 1.0 / math.sqrt(HEAD_DIM)
        scores = jnp.einsum('bqhgd,bkhd->bhgqk', q, k) * scale
        attn = jax.nn.softmax(scores.astype(jnp.float32), axis=-1).astype(q.dtype)
        out = jnp.einsum('bhgqk,bkhd->bqhgd', attn, v)
        out = out.reshape(b, q_len, N_HEADS * HEAD_DIM)
        return out @ Wo

    def _L3_ffn_ref(x, W_base, b_base, W_router, A, B):
        import jax, jax.numpy as jnp
        import numpy as np
        NUM_EXPERTS = 8
        TOP_K = 2
        RANK = 16
        LORA_ALPHA = 32
        SCALING = LORA_ALPHA / RANK
        bs, seq, d_in = x.shape
        T = bs * seq
        xf = x.reshape(T, d_in)
        base = xf @ W_base.T + b_base
        logits = xf @ W_router.T
        rw, sel = jax.lax.top_k(logits, TOP_K)
        rw = jax.nn.softmax(rw, axis=-1)
        onehot = jax.nn.one_hot(sel, NUM_EXPERTS, dtype=rw.dtype)
        w = jnp.einsum('tk,tke->te', rw, onehot)
        h = jnp.einsum('td,erd->ter', xf, A)
        lora = jnp.einsum('ter,te,eor->to', h, w, B) * SCALING
        return (base + lora).reshape(bs, seq, -1)
    x = x + _L0_xattn_ref(_layernorm(x, axis=-1), ctx_4096, mask_1x1xSxS2_ff0, L0_xattn_q_proj_w, L0_xattn_k_proj_w, L0_xattn_v_proj_w, L0_xattn_o_proj_w, L0_xattn_q_norm_w, L0_xattn_k_norm_w)
    x = x + _L0_ffn_ref(_layernorm(x, axis=-1), L0_ffn_weight, L0_ffn_bias, L0_ffn_gate_w, L0_ffn_in_channel_scale, L0_ffn_out_channel_scale)
    x = x + _L1_xattn_ref(_layernorm(x, axis=-1), ctx_4096, L1_xattn_Wq, L1_xattn_bq, L1_xattn_Wk, L1_xattn_bk)
    x = x + _L1_ffn_ref(_layernorm(x, axis=-1), L1_ffn_W_base, L1_ffn_b_base, L1_ffn_enc0, L1_ffn_enc1, L1_ffn_coefs0, L1_ffn_coefs1, L1_ffn_mask0, L1_ffn_mask1)
    x = x + _L2_xattn_ref(_layernorm(x, axis=-1), ctx_4096, mask_BxSxS2_bk0, fside_Bx32xSxS2_0, L2_xattn_Wq, L2_xattn_Wk, L2_xattn_Wv, L2_xattn_Wo)
    x = x + _L2_ffn_ref(_layernorm(x, axis=-1), L2_ffn_W_base, L2_ffn_b_base, L2_ffn_W_gate, L2_ffn_W_thr, L2_ffn_b_thr, L2_ffn_A_w, L2_ffn_B_w)
    x = x + _L3_xattn_ref(_layernorm(x, axis=-1), ctx_4096, L3_xattn_Wq, L3_xattn_Wk, L3_xattn_Wv, L3_xattn_Wo)
    x = x + _L3_ffn_ref(_layernorm(x, axis=-1), L3_ffn_W_base, L3_ffn_b_base, L3_ffn_W_router, L3_ffn_A, L3_ffn_B)
    return x

_drawn_inputs = setup_inputs


def setup_inputs(seed=0):
    import zlib

    import numpy as np

    out = dict(_drawn_inputs(seed))
    spreads = {'L0_xattn_q_norm_w': (1.0, 0.2),
     'L0_xattn_k_norm_w': (1.0, 0.2),
     'L1_xattn_bq': (0.0, 0.8),
     'L1_xattn_bk': (0.0, 0.8)}
    factors = {'L0_ffn_bias': 8.0,
     'L1_ffn_b_base': 8.0,
     'L1_ffn_enc0': 7.93,
     'L1_ffn_enc1': 8.0,
     'L1_ffn_coefs0': 8.0,
     'L1_ffn_coefs1': 8.0,
     'L2_ffn_b_base': 8.0,
     'L3_ffn_b_base': 8.0,
     'L3_ffn_W_router': 6.575,
     'L3_ffn_A': 5.857,
     'L3_ffn_B': 5.8}
    for name, (base, spread) in spreads.items():
        noise = np.random.default_rng([zlib.crc32(name.encode()), seed]).standard_normal(out[name].shape)
        drawn = base * np.exp(spread * noise) if base else spread * noise
        out[name] = jnp.asarray(drawn.astype(out[name].dtype))
    for name, factor in factors.items():
        out[name] = (out[name] * factor).astype(out[name].dtype)
    return out
```

```python
import math
from contextlib import ExitStack

import concourse.bass as bass
from concourse import mybir

FP32 = mybir.dt.float32
FP16 = mybir.dt.float16
BF16 = mybir.dt.bfloat16
U8 = mybir.dt.uint8
U32 = mybir.dt.uint32
ALU = mybir.AluOpType
ACT = mybir.ActivationFunctionType
AX = mybir.AxisListType
RMAX = bass.bass_isa.ReduceOp.max

P = 128
B, S, D = 16, 64, 512
TOK = B * S
TILES = TOK // P
KC = D // P
HG = 4
GROUPS = 8
UNITS = GROUPS * TILES
SCALE = 1.0 / math.sqrt(P)
EPS = 1e-5
LARGE = 1.0e30
FLOOR = 1.0e25
C_W = 2048.0
C_X = 31.0
C_N = 64.0
E8, R16 = 8, 16
R40 = 40


def at(t, per, plus):
    if isinstance(t, int):
        return per * t + plus
    r, d = t
    return r * (2 * per) + (per * d + plus)


class Signal:

    def __init__(self, sem, base=0):
        self.sem, self.base = sem, base

    def by(self, value):
        if isinstance(value, int):
            value = max(value, 0)
        return self.sem, value + self.base


class Chain:

    def __init__(self, signal):
        self.own, self.sem, self.count, self.base, self.per = signal, signal.sem, 0, 0, 0

    def next(self, t=0):
        self.count += 1
        return self.own.by(at(t, self.per, self.base + self.count) if self.per else self.base + self.count)

    def start_periods(self, first, per):
        self.base, self.per, self.count = self.base + self.count - first * per, per, 0

    def next_period(self, check=True):
        assert not check or self.count == self.per, (self.count, self.per)
        self.count = 0

    def end_periods(self, t):
        self.base, self.per = self.base + self.per * t, 0


def mm3(pe, out, lhs, rhs, first=True, last=True):
    pe.matmul(out, lhs[0], rhs[0], start=first, stop=False)
    pe.matmul(out, lhs[0], rhs[1], start=False, stop=False)
    return pe.matmul(out, lhs[1], rhs[0], start=False, stop=last)


def parity(t):
    return (t if isinstance(t, int) else t[1]) % 2


class Attention:

    CHAIN = {"dve": {0: 0, 2: 16, 3: 8}, "pool": {0: 23, 2: 17, 3: 12}}

    def __init__(self, k, layer, dram, before, before_count):
        self.k, self.layer, self.dram = k, layer, dram
        self.before, self.before_count = before, before_count
        self.tiles = {0: ["Q0", "Q1", "Q2", "Q3", "K0", "V0"],
                      2: [f"{w}{h}" for w in "QKV" for h in range(4)],
                      3: [f"Q{h}" for h in range(4)]}[layer]
        self.NT = len(self.tiles)
        self.per_slot = {6: [2, 2, 1, 1], 12: [3] * 4, 4: [1] * 4}[self.NT]
        self.pre = ["q", "k", "v"] if layer != 3 else ["k", "v", "q"]
        self.kinds = {0: ["o", "k", "q", "v"], 2: ["o", "q", "k", "v"], 3: ["o", "q"]}[layer]
        self.NP, self.NK = len(self.pre), len(self.kinds)
        names = ["raw0", "raw1", "w_ss", "w_tot", "w_scale", "w_hi", "w_lo", "misc", "misc_read",
                 "proj", "proj_hi", "proj_lo", "scores", "biased", "top", "exped", "rinv", "probs",
                 "turned", "turned_hi", "turned_lo", "mixed", "mixed_hi", "mixed_lo", "outp", "xadd",
                 "stat", "rstd", "xn", "xt", "xt_hi", "xt_lo", "dve", "pool"]
        names += {0: ["k_tot", "k_rs", "k_n", "k_nhi", "k_nlo", "q_tot", "q_rs"],
                  2: ["bias0", "bias1", "bias_sum", "masks"],
                  3: ["kv", "kv_hi", "kv_lo", "ctx_in", "ctx_hi", "ctx_lo", "kv_scale"]}[layer]
        self.misc_per = self.NK + (6 if layer == 0 else 0)
        slabs = self.NP + 7 * self.NK + 1
        totals = dict.fromkeys(("w_ss", "w_tot", "w_scale", "w_hi", "w_lo"), slabs)
        totals |= {"raw0": 16 * ((slabs + 1) // 2), "raw1": 16 * (slabs // 2), "stat": 1, "rstd": 1}
        totals |= dict.fromkeys(("misc", "misc_read"), self.NP + 7 * self.misc_per + 1 + (6 if layer == 0 else 0))
        totals |= dict.fromkeys(("proj", "proj_hi", "proj_lo"), 16 * self.NT)
        totals |= dict.fromkeys(("xn", "xt", "xt_hi", "xt_lo"), TILES)
        totals |= dict.fromkeys(("scores", "top", "exped", "rinv", "probs", "turned", "turned_hi", "turned_lo",
                                 "mixed", "mixed_hi", "mixed_lo", "outp", "xadd"), UNITS)
        totals |= {"biased": 0 if layer == 3 else UNITS}
        self.s = k.signals(f"a{layer}", names, totals)
        self.own = Chain(self.s["pool"])
        self.ahead = layer != 0

    def events(self, t):
        ok = lambda b: t is None or 0 <= 8 * t + b < UNITS
        kinds = {7: 1, 8: 0}.get(t, self.NK)
        out, tile, misc = [], 0, 0
        for slot in range(8):
            b = slot - 4
            todo = [] if t == 8 else list(range(tile, tile + self.per_slot[slot % 4]))
            tile += len(todo)
            if self.layer == 0:
                made = {1: 0, 2: 1, 5: 2, 6: 3}.get(slot)
                squared = {0: 0, 1: 1, 4: 2, 5: 3}.get(slot)
            else:
                made = slot // 2 if slot % 2 else None
                squared = None if slot % 2 else slot // 2
            made = made if made is not None and made < kinds else None
            squared = squared if squared is not None and squared < kinds else None
            normed = slot % 4 if self.layer == 0 and t != 8 else None
            if ok(b):
                out.append(("scores", b))
            if made is not None:
                out.append(("w_sum", made, misc))
                misc += 1
            if normed == 3:
                out.append(("q_turn", misc, slot // 4))
                misc += 1
                out.append(("k_scale", slot // 4))
            if todo:
                out.append(("tile", todo.pop(0), slot // 4))
            if ok(b):
                out.append(("rinv", b))
            if squared is not None:
                out.append(("w_squares", squared))
            if ok(b - 1):
                out.append(("turn", b - 1))
            if todo:
                out.append(("tile", todo.pop(0), slot // 4))
            if normed == 3:
                out.append(("k_turn", misc, slot // 4))
                misc += 1
            if ok(b - 2):
                out.append(("mix", b - 2))
            if normed == 2:
                out.append(("k_rms", slot // 4))
            if made is not None:
                out.append(("w_convert", made))
            if ok(b - 3):
                out.append(("out", b - 3))
            if todo:
                out.append(("tile", todo.pop(0), slot // 4))
            if normed == 2:
                out.append(("q_sum", misc, slot // 4))
                misc += 1
        return out

    def periods(self, eng, emit, chain=None, per=0):
        emit(0, self.events(0))
        if chain:
            chain.start_periods(1, per)
        with eng.Fori(0, 3) as r:
            for d in (1, 2):
                emit((r, d), self.events(None))
                if chain:
                    chain.next_period()
        emit(7, self.events(7))
        if chain:
            chain.next_period(False)
        emit(8, self.events(8))
        if chain:
            chain.end_periods(8)

    def group(self, t, b):
        return (parity(t) + b // 8) % 2

    def slab(self, kind, par, part):
        k = self.k
        if kind == "o":
            return k.wo[:, par, part]
        if kind == "q" or self.layer == 2:
            return k.wproj[:, "qkv".index(kind), par, part]
        if self.layer == 0:
            return k.wsmall[:, "qkv".index(kind) - 1, par, part]
        return k.wproj[:, 0, 1, part] if kind == "k" else k.wo[:, 1, part]

    def raw(self, j, kind):
        if self.layer == 0 and kind in "kv":
            return self.k.raw[:, j % 2, 0:512].rearrange("p (c n) -> p c n", c=KC)
        return self.k.raw[:, j % 2, :].rearrange("p (c n) -> p c n", c=KC)

    def xt(self, part, c, lo, n):
        return self.k.xt[:, part, c, lo:lo + n]

    def load(self, sp, kind, g, j, free):
        k, s = self.k, self.s
        sp.wait_ge(*s["w_lo"].by(free))
        src = self.dram[kind]
        if kind in "kv" and self.layer == 3:
            src = src[0]
        elif isinstance(g, int):
            src = src[g]
        else:
            src = src[bass.ds(g, 1)].rearrange("o p n -> (o p) n")
        dst = k.raw[:, j % 2, 0:src.shape[-1]]
        sp.dma_start(dst, src).then_inc((s["raw0"], s["raw1"])[j % 2].sem, 16)

    def sp_ahead(self, sp):
        if self.layer == 2:
            sp.dma_start(self.k.mask_u8[:, :, :], self.dram["mask"]).then_inc(self.s["masks"].sem, 16)
        for j, kind in enumerate(self.pre):
            self.load(sp, kind, 0, j, j - 1)

    def sp(self, sp):
        k, s = self.k, self.s
        if not self.ahead:
            self.sp_ahead(sp)
        if self.layer == 3:
            sp.wait_ge(*self.before.by(self.before_count))
            sp.dma_start(k.ctx_in[:, :, :], self.dram["ctx_t"]).then_inc(s["ctx_in"].sem, 16)

        def bias(t, b):
            if isinstance(t, int):
                n = 8 * t + b
                src = self.dram["bias"][n]
                free = n - 1
            else:
                n = at(t, 8, b)
                src = self.dram["bias"][bass.ds(n, 1)].rearrange("o p n -> (o p) n")
                free = at(t, 8, b - 1)
            sp.wait_ge(*s["biased"].by(free))
            sp.dma_start(k.bias_in[:, b % 2, :], src).then_inc((s["bias0"], s["bias1"])[b % 2].sem, 16)

        def emit(t, events):
            kinds = {7: 1, 8: 0}.get(t, self.NK) if isinstance(t, int) else self.NK
            for slot in range(8):
                if self.layer == 2 and (not isinstance(t, int) or 0 <= 8 * t + slot - 4 < UNITS):
                    bias(t, slot - 4)
                if slot % 2 == 0 and slot // 2 < kinds:
                    n, kind = slot // 2, self.kinds[slot // 2]
                    g = at(t, 1, 0 if kind == "o" else 1)
                    self.load(sp, kind, g, self.NP + self.NK * 0 + n + (self.NK * parity(t)),
                         at(t, self.NK, self.NP + n - 1))

        self.periods(sp, emit)

    def squares(self, act, kind, j, par, raw_count, free=None):
        s = self.s
        if free:
            act.wait_ge(*free[0].by(free[1]))
        act.wait_ge(*(s["raw0"], s["raw1"])[j % 2].by(raw_count))
        junk = self.slab(kind, par, 0).bitcast(BF16)
        act.activation(junk, self.raw(j, kind), ACT.Square,
                       accum_out=self.k.w_ss[:, j % 2:j % 2 + 1]).then_inc(s["w_ss"].sem, 1)

    def high(self, act, kind, j, par, count):
        act.wait_ge(*self.s["w_scale"].by(count))
        act.activation(self.slab(kind, par, 0), self.raw(j, kind), ACT.Copy,
                       scale=self.k.w_scale[:, j % 2:j % 2 + 1]).then_inc(self.s["w_hi"].sem, 1)

    def squares_ahead(self, act, j):
        self.squares(act, self.pre[j], j, 0, 16 * (j // 2 + 1))

    def high_ahead(self, act, j):
        self.high(act, self.pre[j], j, 0, j + 1)

    def act_ahead(self, act):
        self.squares_ahead(act, 0)
        for j in range(self.NP):
            if j + 1 < self.NP:
                self.squares_ahead(act, j + 1)
            self.high_ahead(act, j)

    def act(self, act):
        k, s = self.k, self.s
        bank = k.bank
        act.wait_ge(*self.before.by(self.before_count))
        if not self.ahead:
            self.act_ahead(act)

        if self.layer == 3:
            act.wait_ge(*s["ctx_in"].by(16))
            act.wait_ge(*s["kv_scale"].by(1))
            for h in range(4):
                act.activation(k.hid_ctx(0, h), k.ctx_in_view(h), ACT.Copy,
                               scale=k.joint[:, 0:1]).then_inc(s["ctx_hi"].sem, 1)
        for t in range(TILES):
            act.wait_ge(*s["xt"].by(t + 1))
            if self.layer == 3:
                act.activation(k.hid_lat(0, t), bank[t % 2][:, :].rearrange("p (c b n) -> p c b n", c=KC, b=2),
                               ACT.Copy).then_inc(s["xt_hi"].sem, 1)
            else:
                act.activation(k.xt[:, 0, :, t * P:(t + 1) * P],
                               bank[t % 2][:, :].rearrange("p (c n) -> p c n", c=KC),
                               ACT.Copy).then_inc(s["xt_hi"].sem, 1)
        if self.layer == 3:
            for m in range(32):
                act.wait_ge(*s["kv"].by(m + 1))
                act.activation(k.kv3(m, 0), bank[m % 2][:, :], ACT.Copy).then_inc(s["kv_hi"].sem, 1)

        def emit(t, events):
            for e in events:
                if e[0] == "w_squares":
                    n, kind = e[1], self.kinds[e[1]]
                    jl = self.NP + n + self.NK * parity(t)
                    if kind == "o":
                        par, free = parity(t), (s["outp"], at(t, 8, -7))
                        if self.layer == 3 and par:
                            act.wait_ge(*s["kv"].by(32))
                    else:
                        par, free = 1 - parity(t), (s["proj"], at(t, 2 * self.NT, 0))
                        if self.layer == 3:
                            act.wait_ge(*s["kv"].by(32))
                    if self.NK % 2 == 0:
                        raw_count = at(t, 8 * self.NK, 16 * ((self.NP + n) // 2 + 1))
                    self.squares(act, kind, jl, par, raw_count, free)
                elif e[0] == "w_convert":
                    n, kind = e[1], self.kinds[e[1]]
                    par = parity(t) if kind == "o" else 1 - parity(t)
                    self.high(act, kind, self.NP + n + self.NK * parity(t), par, at(t, self.NK, self.NP + n + 1))
                elif e[0] == "tile":
                    _, m, part = e
                    name = self.tiles[m - self.NT * part]
                    count = at(t, 2 * self.NT, m + 1)
                    src = bank[m % 2][:, :]
                    if name[0] in "QK":
                        act.wait_ge(*s["scores"].by(at(t, 8, 4 * part - 4)))
                    else:
                        act.wait_ge(*s["mixed"].by(at(t, 8, 4 * part - 4)))
                    if self.layer == 0 and name == "K0":
                        act.wait_ge(*s["k_tot"].by(at(t, 2, part)))
                        act.wait_ge(*s["proj"].by(count))
                        for tt in range(4):
                            ins = act.activation(k.ksq[:, tt * P:(tt + 1) * P], src[:, tt * P:(tt + 1) * P],
                                                 ACT.Square, accum_out=k.ksum[:, tt:tt + 1])
                        ins.then_inc(s["proj_hi"].sem, 1)
                        continue
                    if self.layer == 0 and name[0] == "Q":
                        if name == "Q0":
                            act.wait_ge(*s["q_tot"].by(at(t, 2, part)))
                        act.wait_ge(*s["proj"].by(count))
                        act.activation(k.qsq[:, int(name[1]), :], src, ACT.Square)
                        act.activation(k.q_parts[:, 0, int(name[1]), :], src, ACT.Square)
                    act.wait_ge(*s["proj"].by(count))
                    act.activation(self.dest(name, part, 0), self.shaped(src), ACT.Copy).then_inc(s["proj_hi"].sem, 1)
                elif e[0] == "k_turn":
                    _, misc, part = e
                    act.wait_ge(*s["misc"].by(at(t, self.misc_per, self.NP + misc + 1)))
                    act.activation(k.dest("K0", part, 0), bank[7][:, :], ACT.Copy,
                                   scale=k.wqk[:, 0:1]).then_inc(s["k_nhi"].sem, 1)
                elif e[0] == "q_sum":
                    _, misc, part = e
                    act.wait_ge(*s["misc"].by(at(t, self.misc_per, self.NP + misc + 1)))
                    act.activation(k.qrow[:, :], bank[7][:, :], ACT.Copy).then_inc(s["misc_read"].sem, 1)
                elif e[0] == "scores":
                    b = e[1]
                    act.wait_ge(*s["top"].by(at(t, 8, b + 1)))
                    act.wait_ge(*s["turned"].by(at(t, 8, b - 1)))
                    for h in range(HG):
                        cols = slice(h * P, (h + 1) * P)
                        if self.layer == 3:
                            qk = k.qk[:, self.group(t, b):self.group(t, b) + 1]
                            ins = act.activation(k.E[:, b % 2, cols], bank[2 + b % 2][:, cols], ACT.Exp,
                                                 bias=k.nmax2[:, b % 2, h:h + 1], scale=qk,
                                                 accum_out=k.rsum[:, b % 2, h:h + 1])
                        else:
                            ins = act.activation(k.E[:, b % 2, cols], k.Sm[:, b % 2, cols], ACT.Exp,
                                                 bias=k.nmax[:, b % 2, h:h + 1],
                                                 accum_out=k.rsum[:, b % 2, h:h + 1])
                    ins.then_inc(s["exped"].sem, 1)
                elif e[0] == "turn":
                    b = e[1]
                    act.wait_ge(*s["turned"].by(at(t, 8, b + 1)))
                    act.wait_ge(*s["mixed"].by(at(t, 8, b - 1)))
                    act.activation(k.PT[:, b % 2, 0, :], bank[4][:, :], ACT.Copy).then_inc(s["turned_hi"].sem, 1)
                elif e[0] == "mix":
                    b = e[1]
                    act.wait_ge(*s["mixed"].by(at(t, 8, b + 1)))
                    act.wait_ge(*s["outp"].by(at(t, 8, b - 1)))
                    act.activation(self.mix_dst(b, 0), self.mix_src(), ACT.Copy).then_inc(s["mixed_hi"].sem, 1)

        self.periods(act, emit)

    def dest(self, name, part, i):
        if self.layer == 3:
            h = int(name[1])
            return self.k.q3[:, i, part, h // 2, :, h % 2, :]
        return self.k.dest(name, part, i)

    def shaped(self, src):
        return src.rearrange("p (b n) -> p b n", b=8) if self.layer == 3 else src

    def mix_src(self):
        if self.layer == 3:
            return self.k.bank[5][:, :].rearrange("p (b h n) -> p b h n", b=2, h=HG)
        return self.k.bank[5][:, :]

    def mix_dst(self, b, part):
        a = self.k.A[:, b % 2, part, :]
        if self.layer == 3:
            return a.rearrange("p (h b n) -> p b h n", b=2, h=HG)
        return a

    def sum_squares(self, pe, j, ss_count, free):
        k, s = self.k, self.s
        pe.wait_ge(*s["misc_read"].by(free))
        pe.wait_ge(*s["w_ss"].by(ss_count))
        pe.matmul(k.bank[7][:, 0:1], k.ones[:, :], k.w_ss[:, j % 2:j % 2 + 1],
                  start=True, stop=True).then_inc(s["misc"].sem, 1)

    def sum_ahead(self, pe, j):
        self.sum_squares(pe, j, j + 1, j)

    def pe(self, pe):
        k, s, bank = self.k, self.s, self.k.bank
        pe.wait_ge(*self.before.by(self.before_count))
        if not self.ahead:
            for j in range(self.NP):
                self.sum_ahead(pe, j)
        for t in range(TILES):
            pe.wait_ge(*s["xn"].by(t + 1))
            pe.wait_ge(*s["xt_lo"].by(t - 1))
            for c in range(KC):
                ins = pe.transpose(bank[t % 2][:, c * P:(c + 1) * P], k.Sm[:, t % 2, c * P:(c + 1) * P], k.ident[:, :])
            ins.then_inc(s["xt"].sem, 1)
        pe.wait_ge(*s["xt_lo"].by(TILES))
        if self.layer == 3:
            pe.wait_ge(*s["w_lo"].by(2))
            pe.wait_ge(*s["ctx_lo"].by(4))
            for m in range(32):
                pe.wait_ge(*s["kv_lo"].by(m - 1))
                for c in range(KC):
                    if m < 16:
                        kvh, q4 = m // 4, m % 4
                        lhs = [self.slab("k", 0, i)[:, c, kvh * P:(kvh + 1) * P] for i in range(2)]
                        rhs = [k.hid[:, i, c, q4 * 4:q4 * 4 + 4, :] for i in range(2)]
                    else:
                        b = m - 16
                        lhs = [k.hid[:, i, c, b, :] for i in range(2)]
                        rhs = [self.slab("v", 0, i)[:, c, :] for i in range(2)]
                    ins = mm3(pe, bank[m % 2][:, :], lhs, rhs, c == 0, c == KC - 1)
                ins.then_inc(s["kv"].sem, 1)
            pe.wait_ge(*s["kv_lo"].by(32))

        def emit(t, events):
            par = parity(t)
            for e in events:
                if e[0] == "w_sum":
                    _, n, misc = e
                    self.sum_squares(pe, self.NP + n + self.NK * par, at(t, self.NK, self.NP + n + 1),
                                     at(t, self.misc_per, self.NP + misc))
                elif e[0] == "tile":
                    _, m, part = e
                    name = self.tiles[m - self.NT * part]
                    if m == 0:
                        pe.wait_ge(*s["w_lo"].by(at(t, self.NK, self.NP - (self.layer != 3))))
                    if name == "V0":
                        pe.wait_ge(*s["w_lo"].by(at(t, self.NK, self.NP)))
                    pe.wait_ge(*s["proj_lo"].by(at(t, 2 * self.NT, m - 1)))
                    h = int(name[1])
                    if name[0] in "KV" and self.layer == 0:
                        for tt in range(4):
                            for c in range(KC):
                                lhs = [k.ct[:, i, c, (part * 4 + tt) * P:(part * 4 + tt + 1) * P] for i in range(2)]
                                rhs = [self.slab(name[0].lower(), par, i)[:, c, :] for i in range(2)]
                                ins = mm3(pe, bank[m % 2][:, tt * P:(tt + 1) * P], lhs, rhs, c == 0, c == KC - 1)
                        ins.then_inc(s["proj"].sem, 1)
                        continue
                    for c in range(KC):
                        if name[0] == "V":
                            lhs = [k.ct[:, i, c, (part * 4 + h) * P:(part * 4 + h + 1) * P] for i in range(2)]
                            rhs = [self.slab("v", par, i)[:, c, :] for i in range(2)]
                        else:
                            kind = name[0].lower()
                            lhs = [self.slab(kind, par, i)[:, c, h * P:(h + 1) * P] for i in range(2)]
                            if self.layer == 3:
                                rhs = [k.hid[:, i, c, part * 8:part * 8 + 8, S:2 * S] for i in range(2)]
                            else:
                                src = k.xt if kind == "q" else k.ct
                                rhs = [src[:, i, c, part * 512:(part + 1) * 512] for i in range(2)]
                        ins = mm3(pe, bank[m % 2][:, :], lhs, rhs, c == 0, c == KC - 1)
                    ins.then_inc(s["proj"].sem, 1)
                elif e[0] == "k_turn":
                    _, misc, part = e
                    pe.wait_ge(*s["misc_read"].by(at(t, self.misc_per, self.NP + misc)))
                    pe.wait_ge(*s["k_n"].by(at(t, 2, part + 1)))
                    for tt in range(4):
                        ins = pe.transpose(bank[7][:, tt * P:(tt + 1) * P], k.kraw[:, tt * P:(tt + 1) * P], k.ident[:, :])
                    ins.then_inc(s["misc"].sem, 1)
                elif e[0] == "q_sum":
                    _, misc, part = e
                    pe.wait_ge(*s["misc_read"].by(at(t, self.misc_per, self.NP + misc)))
                    pe.wait_ge(*s["proj_lo"].by(at(t, 2 * self.NT, self.NT * part + HG)))
                    for h in range(HG):
                        for i in range(2):
                            ins = pe.matmul(bank[7][:, :], k.select[:, h, :], k.q_parts[:, i, h, :],
                                            start=h + i == 0, stop=h + i == HG)
                    ins.then_inc(s["misc"].sem, 1)
                elif e[0] == "q_turn":
                    _, misc, part = e
                    pe.wait_ge(*s["misc_read"].by(at(t, self.misc_per, self.NP + misc)))
                    for tt in range(4):
                        ins = pe.transpose(bank[7][:, tt * P:(tt + 1) * P], k.qrow[:, tt * P:(tt + 1) * P],
                                           k.ident[:, :])
                    ins.then_inc(s["misc"].sem, 1)
                elif e[0] == "scores":
                    b = e[1]
                    hf, pt = (b // 4) % 2, b % 4
                    pe.wait_ge(*(s["exped"] if self.layer == 3 else s["biased"]).by(at(t, 8, b - 1)))
                    out = bank[2 + b % 2]
                    if b % 4 == 0:
                        need = {0: 5, 2: 8, 3: 4}[self.layer]
                        pe.wait_ge(*s["proj_lo"].by(at(t, 2 * self.NT, self.NT * (b // 4) + need)))
                        if self.layer == 0:
                            pe.wait_ge(*s["k_nlo"].by(at(t, 2, b // 4 + 1)))
                    for j in range(4):
                        if self.layer == 3:
                            b2, hp = j // 2, j % 2
                            lhs = [k.q3[:, i, hf, hp, pt * 2 + b2].rearrange("p h n -> p (h n)") for i in range(2)]
                            rhs = [self.keys3(t, b, i, b2) for i in range(2)]
                        else:
                            kh = 0 if self.layer == 0 else j
                            lhs = [k.Q[:, i, hf, j, pt * P:(pt + 1) * P] for i in range(2)]
                            rhs = [k.K[:, i, hf, kh, pt * P:(pt + 1) * P] for i in range(2)]
                        ins = mm3(pe, out[:, j * P:(j + 1) * P], lhs, rhs)
                    ins.then_inc(s["scores"].sem, 1)
                elif e[0] == "turn":
                    b = e[1]
                    pe.wait_ge(*s["turned_lo"].by(at(t, 8, b)))
                    pe.wait_ge(*s["probs"].by(at(t, 8, b + 1)))
                    for j in range(4):
                        ins = pe.transpose(bank[4][:, j * P:(j + 1) * P], k.E[:, b % 2, j * P:(j + 1) * P], k.ident[:, :])
                    ins.then_inc(s["turned"].sem, 1)
                elif e[0] == "mix":
                    b = e[1]
                    hf, pt = (b // 4) % 2, b % 4
                    pe.wait_ge(*s["mixed_lo"].by(at(t, 8, b)))
                    pe.wait_ge(*s["turned_lo"].by(at(t, 8, b + 1)))
                    if b % 4 == 0 and self.layer != 3:
                        pe.wait_ge(*s["proj_lo"].by(at(t, 2 * self.NT, self.NT * (b // 4) + self.NT)))
                    out = bank[5]
                    pt_ = k.PT[:, b % 2]
                    if self.layer == 0:
                        lhs = [k.V[:, i, hf, 0, pt * P:(pt + 1) * P] for i in range(2)]
                        ins = mm3(pe, out[:, :], lhs, [pt_[:, i, :] for i in range(2)])
                    elif self.layer == 2:
                        for h in range(4):
                            cols = slice(h * P, (h + 1) * P)
                            ins = mm3(pe, out[:, cols], [k.V[:, i, hf, pt, cols] for i in range(2)],
                                      [pt_[:, i, cols] for i in range(2)])
                    else:
                        for b2 in range(2):
                            cols = slice(b2 * 256, (b2 + 1) * 256)
                            ins = mm3(pe, out[:, cols], [self.values3(t, b, i, b2) for i in range(2)],
                                      [pt_[:, i, cols] for i in range(2)])
                    ins.then_inc(s["mixed"].sem, 1)
                elif e[0] == "out":
                    b = e[1]
                    g = self.group(t, b)
                    pe.wait_ge(*s["xadd"].by(at(t, 8, b)))
                    pe.wait_ge(*s["mixed_lo"].by(at(t, 8, b + 1)))
                    if b % 8 == 0:
                        pe.wait_ge(*s["w_lo"].by(at(t, self.NK, self.NP + self.NK * (b // 8) + 1)))
                    for h in range(4):
                        ins = mm3(pe, bank[6][:, :], [k.A[:, b % 2, i, h * P:(h + 1) * P] for i in range(2)],
                                  [self.slab("o", g, i)[:, h, :] for i in range(2)], h == 0, h == 3)
                    ins.then_inc(s["outp"].sem, 1)

        self.periods(pe, emit)

    def kvh(self, t, b):
        if isinstance(t, int):
            return (t + b // 8) // 2
        return t[0] + (t[1] + b // 8) // 2

    def keys3(self, t, b, i, b2):
        kvh, bat = self.kvh(t, b), 2 * (b % 8) + b2
        if isinstance(kvh, int):
            return self.k.kt3[:, i, kvh, bat, :]
        return self.k.kt3[:, i, bass.ds(kvh, 1), bat, :].rearrange("p o n -> p (o n)")

    def values3(self, t, b, i, b2):
        kvh, bat = self.kvh(t, b), 2 * (b % 8) + b2
        if isinstance(kvh, int):
            return self.k.v3[:, i, bat, kvh, :]
        return self.k.v3[:, i, bat, bass.ds(kvh, 1), :].rearrange("p o n -> p (o n)")

    def total(self, dve, j, count):
        k, s = self.k, self.s
        dve.wait_ge(*s["misc"].by(count))
        dve.tensor_scalar(k.w_tot[:, j % 2:j % 2 + 1], k.bank[7][:, 0:1], 1e-30, None, ALU.add)\
           .then_inc(s["misc_read"].sem, 1)

    def low(self, dve, kind, j, par, count):
        dve.wait_ge(*self.s["w_hi"].by(count))
        dve.scalar_tensor_tensor(out=self.slab(kind, par, 1), in0=self.raw(j, kind),
                                 scalar=self.k.w_scale[:, j % 2:j % 2 + 1], in1=self.slab(kind, par, 0),
                                 op0=ALU.mult, op1=ALU.subtract).then_inc(self.s["w_lo"].sem, 1)

    def total_ahead(self, dve, j):
        self.total(dve, j, j + 1)

    def low_ahead(self, dve, j):
        self.low(dve, self.pre[j], j, 0, j + 1)

    def dve(self, dve):
        k, s, bank = self.k, self.s, self.k.bank
        ch = Chain(s["dve"])
        dve.wait_ge(*self.before.by(self.before_count))
        k.ln_stats(dve, ch, s)
        if not self.ahead:
            for j in range(self.NP):
                self.total_ahead(dve, j)
                self.low_ahead(dve, j)
        if self.layer == 2:
            dve.wait_ge(*s["masks"].by(16))
            dve.tensor_scalar(k.mask2[:, :, :], k.mask_u8[:, :, :], -1.0, LARGE, ALU.add, ALU.mult)\
               .then_inc(s["masks"].sem, 1)
        if self.layer == 3:
            dve.wait_ge(*s["kv_scale"].by(1))
            for h in range(4):
                dve.wait_ge(*s["ctx_hi"].by(h + 1))
                dve.scalar_tensor_tensor(out=k.hid_ctx(1, h), in0=k.ctx_in_view(h),
                                         scalar=k.joint[:, 0:1], in1=k.hid_ctx(0, h),
                                         op0=ALU.mult, op1=ALU.subtract).then_inc(s["ctx_lo"].sem, 1)
        dve.wait_ge(*s["rstd"].by(1))

        def norm(t):
            dve.wait_ge(*s["xt"].by(t - 1))
            dve.tensor_scalar(k.Sm[:, t % 2, :], k.x[:, t, :], k.mv[:, t, 0:1], k.rstd[:, t:t + 1],
                              ALU.subtract, ALU.mult).then_inc(s["xn"].sem, 1)

        norm(0)
        for t in range(TILES):
            if t + 1 < TILES:
                norm(t + 1)
            dve.wait_ge(*s["xt_hi"].by(t + 1))
            if self.layer == 3:
                dve.tensor_tensor(k.hid_lat(1, t),
                                  bank[t % 2][:, :].rearrange("p (c b n) -> p c b n", c=KC, b=2),
                                  k.hid_lat(0, t), ALU.subtract).then_inc(s["xt_lo"].sem, 1)
            else:
                dve.tensor_tensor(k.xt[:, 1, :, t * P:(t + 1) * P],
                                  bank[t % 2][:, :].rearrange("p (c n) -> p c n", c=KC),
                                  k.xt[:, 0, :, t * P:(t + 1) * P], ALU.subtract).then_inc(s["xt_lo"].sem, 1)
        if self.layer == 2:
            dve.wait_ge(*s["xt"].by(TILES))
            dve.memset(k.Sm[:, :, :], -LARGE).then_inc(ch.sem, 1)
            dve.wait_ge(*ch.next())
        if self.layer == 3:
            for m in range(32):
                dve.wait_ge(*s["kv_hi"].by(m + 1))
                dve.tensor_tensor(k.kv3(m, 1), bank[m % 2][:, :], k.kv3(m, 0), ALU.subtract).then_inc(s["kv_lo"].sem, 1)

        def emit(t, events):
            par = parity(t)
            for e in events:
                if e[0] == "w_sum":
                    _, n, misc = e
                    self.total(dve, self.NP + n + self.NK * par, at(t, self.misc_per, self.NP + misc + 1))
                elif e[0] == "w_convert":
                    n, kind = e[1], self.kinds[e[1]]
                    self.low(dve, kind, self.NP + n + self.NK * par, par if kind == "o" else 1 - par,
                        at(t, self.NK, self.NP + n + 1))
                elif e[0] == "tile":
                    _, m, part = e
                    name = self.tiles[m - self.NT * part]
                    dve.wait_ge(*s["proj_hi"].by(at(t, 2 * self.NT, m + 1)))
                    if self.layer == 0 and name == "K0":
                        dve.wait_ge(*s["k_nlo"].by(at(t, 2, part)))
                        dve.tensor_copy(k.kraw[:, :], bank[m % 2][:, :]).then_inc(s["proj_lo"].sem, 1)
                    else:
                        ins = dve.tensor_tensor(self.dest(name, part, 1), self.shaped(bank[m % 2][:, :]),
                                                self.dest(name, part, 0), ALU.subtract)
                        if self.layer == 0 and name[0] == "Q":
                            h = int(name[1])
                            ins = dve.tensor_tensor(k.q_parts[:, 1, h, :], k.qsq[:, h, :], k.q_parts[:, 0, h, :],
                                                    ALU.subtract)
                        ins.then_inc(s["proj_lo"].sem, 1)
                elif e[0] == "k_rms":
                    part = e[1]
                    dve.wait_ge(*s["proj_hi"].by(at(t, 2 * self.NT, self.NT * part + HG + 1)))
                    dve.wait_ge(*s["k_rs"].by(at(t, 2, part)))
                    dve.tensor_scalar(k.ktot[:, :], k.ksum[:, :], 1.0 / P, k.eps_k[:, par:par + 1],
                                      ALU.mult, ALU.add).then_inc(s["k_tot"].sem, 1)
                elif e[0] == "k_scale":
                    part = e[1]
                    dve.wait_ge(*s["k_rs"].by(at(t, 2, part + 1)))
                    dve.wait_ge(*s["proj_lo"].by(at(t, 2 * self.NT, self.NT * part + HG + 1)))
                    kr = k.kraw[:, :].rearrange("p (t n) -> p t n", t=4)
                    dve.tensor_tensor(kr, kr, bc(k.krs[:, :], P), ALU.mult).then_inc(s["k_n"].sem, 1)
                elif e[0] == "k_turn":
                    _, misc, part = e
                    dve.wait_ge(*s["k_nhi"].by(at(t, 2, part + 1)))
                    dve.scalar_tensor_tensor(out=k.dest("K0", part, 1), in0=bank[7][:, :], scalar=k.wqk[:, 0:1],
                                             in1=k.dest("K0", part, 0), op0=ALU.mult,
                                             op1=ALU.subtract).then_inc(s["k_nlo"].sem, 1)
                    dve.wait_ge(*s["k_nlo"].by(at(t, 2, part + 1)))
                    dve.tensor_copy(k.peak[:, 5:6], k.peak[:, 4:5]).then_inc(s["misc_read"].sem, 1)
                elif e[0] == "q_turn":
                    _, misc, part = e
                    dve.wait_ge(*s["misc"].by(at(t, self.misc_per, self.NP + misc + 1)))
                    dve.wait_ge(*s["q_rs"].by(at(t, 2, part)))
                    dve.tensor_scalar(k.qtot[:, :].rearrange("p (t h) -> p t h", t=4),
                                      bank[7][:, :].rearrange("p (t n) -> p t n", t=4)[:, :, 0:HG], 1.0 / P, k.eps_q[:, par:par + 1],
                                      ALU.mult, ALU.add).then_inc(s["q_tot"].sem, 1)
                    dve.wait_ge(*s["q_tot"].by(at(t, 2, part + 1)))
                    dve.tensor_copy(k.qtot2[:, :], k.qtot[:, :]).then_inc(s["misc_read"].sem, 1)
                elif e[0] == "scores":
                    b = e[1]
                    i2, g = b % 2, self.group(t, b)
                    pair = b % 8
                    dve.wait_ge(*s["scores"].by(at(t, 8, b + 1)))
                    src = bank[2 + i2]
                    if self.layer == 3:
                        dve.wait_ge(*s["exped"].by(at(t, 8, b - 1)))
                        dve.tensor_reduce(k.nmax[:, i2, :], src[:, :].rearrange("p (h n) -> p h n", h=HG),
                                          AX.X, ALU.max, negate=True).then_inc(ch.sem, 1)
                        dve.wait_ge(*ch.next(t))
                        dve.tensor_scalar(k.nmax2[:, i2, :], k.nmax[:, i2, :], k.qk[:, g:g + 1], None, ALU.mult)\
                           .then_inc(s["top"].sem, 1)
                        continue
                    dve.wait_ge(*s["exped"].by(at(t, 8, b - 1)))
                    if self.layer == 0:
                        if b % 4 == 0:
                            dve.wait_ge(*s["q_rs"].by(at(t, 2, b // 4 + 1)))
                        hf = (b // 4) % 2
                        for h in range(HG):
                            cols = slice(h * P, (h + 1) * P)
                            i = (b % 4) * HG + h
                            ins = dve.scalar_tensor_tensor(out=k.Sm[:, i2, cols], in0=src[:, cols],
                                                           scalar=k.rq[:, hf, i:i + 1], in1=k.mask0[:, :],
                                                           op0=ALU.mult, op1=ALU.add)
                        ins.then_inc(s["biased"].sem, 1)
                    else:
                        dve.wait_ge(*s["bias_sum"].by(at(t, 8, b + 1)))
                        blk = lambda v, q, n: v[q * S:(q + 1) * S, :].rearrange("p (h n) -> p h n", h=HG)[:, :, n]
                        for q in range(2):
                            own = slice(q * S, (q + 1) * S)
                            ins = dve.scalar_tensor_tensor(
                                out=blk(k.Sm[:, i2, :], q, own), in0=blk(src, q, own),
                                scalar=k.qk[own, g:g + 1], in1=blk(k.bias_in[:, i2, :], q, slice(0, S)),
                                op0=ALU.mult, op1=ALU.add)
                        ins.then_inc(s["biased"].sem, 1)
                    dve.wait_ge(*s["biased"].by(at(t, 8, b + 1)))
                    ins = dve.tensor_reduce(k.nmax[:, i2, :], k.Sm[:, i2, :].rearrange("p (h n) -> p h n", h=HG),
                                            AX.X, ALU.max, negate=True)
                    if self.layer == 2:
                        ins.then_inc(ch.sem, 1)
                        dve.wait_ge(*ch.next(t))
                        ins = dve.tensor_scalar(k.nmax[:, i2, :], k.nmax[:, i2, :], FLOOR, None, ALU.min)
                    ins.then_inc(s["top"].sem, 1)
                elif e[0] == "rinv":
                    b = e[1]
                    i2 = b % 2
                    dve.wait_ge(*s["exped"].by(at(t, 8, b + 1)))
                    dve.wait_ge(*s["probs"].by(at(t, 8, b - 1)))
                    if self.layer == 2:
                        dve.tensor_scalar(k.rsum[:, i2, :], k.rsum[:, i2, :], 1e-30, None, ALU.max).then_inc(ch.sem, 1)
                        dve.wait_ge(*ch.next(t))
                    dve.reciprocal(k.rinv[:, i2, :], k.rsum[:, i2, :]).then_inc(s["rinv"].sem, 1)
                elif e[0] == "turn":
                    b = e[1]
                    dve.wait_ge(*s["turned_hi"].by(at(t, 8, b + 1)))
                    dve.tensor_tensor(k.PT[:, b % 2, 1, :], bank[4][:, :], k.PT[:, b % 2, 0, :],
                                      ALU.subtract).then_inc(s["turned_lo"].sem, 1)
                elif e[0] == "mix":
                    b = e[1]
                    dve.wait_ge(*s["mixed_hi"].by(at(t, 8, b + 1)))
                    dve.tensor_tensor(self.mix_dst(b, 1), self.mix_src(), self.mix_dst(b, 0),
                                      ALU.subtract).then_inc(s["mixed_lo"].sem, 1)
                elif e[0] == "out":
                    b = e[1]
                    g, pair = self.group(t, b), b % 8
                    dve.wait_ge(*s["outp"].by(at(t, 8, b + 1)))
                    dve.scalar_tensor_tensor(out=k.x[:, pair, :], in0=bank[6][:, :], scalar=k.osc[:, g:g + 1],
                                             in1=k.x[:, pair, :], op0=ALU.mult, op1=ALU.add).then_inc(s["xadd"].sem, 1)

        self.periods(dve, emit, ch, self.CHAIN["dve"][self.layer])

    def tt(self, pool, out, a, b, op, t=0, sem=None):
        if sem is None:
            pool.tensor_tensor(out, a, b, op).then_inc(self.own.sem, 1)
            pool.wait_ge(*self.own.next(t))
        else:
            pool.tensor_tensor(out, a, b, op).then_inc(sem.sem, 1)

    def scales(self, pool, kind, j, par, count, t=0):
        k, s = self.k, self.s

        def tt(*args):
            self.tt(pool, *args)

        pool.wait_ge(*s["misc_read"].by(count))
        i = slice(j % 2, j % 2 + 1)
        tot, sc = k.w_tot[:, i], k.w_scale[:, i]
        kp = slice(par, par + 1)
        inv = k.inv["qkvo".index(kind)][:, kp]
        tt(sc, tot, k.c_mhalf, ALU.pow, t)
        tt(inv, tot, k.c_half, ALU.pow, t)
        tt(inv, inv, k.c_icw, ALU.mult, t)
        last = lambda: tt(sc, sc, k.c_cw, ALU.mult, t, s["w_scale"])
        if self.layer == 0 and kind in "qk":
            tt(k.tmp, sc, k.c_cw, ALU.mult, t)
            if kind == "k":
                tt(k.tmp, k.tmp, k.s_c[:, 0:1], ALU.mult, t)
            tt(k.tmp, k.tmp, k.tmp, ALU.mult, t)
            tt((k.eps_q if kind == "q" else k.eps_k)[:, kp], k.tmp, k.c_eps, ALU.mult, t)
        if self.layer == 2 and kind == "k":
            tt(k.tmp, inv, k.inv[0][:, kp], ALU.mult, t)
            tt(k.tmp, k.tmp, k.inv_c[:, 0:1], ALU.mult, t)
            tt(k.qk[:, kp], k.tmp, k.c_scale, ALU.mult, t)
        if self.layer == 3 and kind == "q":
            tt(k.tmp, inv, k.inv[1][:, 0:1], ALU.mult, t)
            tt(k.tmp, k.tmp, k.joint[:, 1:2], ALU.mult, t)
            tt(k.tmp, k.tmp, k.joint[:, 1:2], ALU.mult, t)
            tt(k.qk[:, kp], k.tmp, k.c_scale, ALU.mult, t)
        if kind == "o":
            if self.layer == 3:
                tt(k.tmp, inv, k.inv[2][:, 0:1], ALU.mult, t)
                tt(k.osc[:, kp], k.tmp, k.joint[:, 1:2], ALU.mult, t)
            else:
                tt(k.tmp, inv, k.inv[2][:, kp], ALU.mult, t)
                tt(k.osc[:, kp], k.tmp, k.inv_c[:, 0:1], ALU.mult, t)
        last()

    def pool_ahead(self, pool):
        k, s = self.k, self.s

        def tt(*args):
            self.tt(pool, *args)

        if self.layer == 3:
            a, b = k.joint[:, 0:1], k.joint[:, 1:2]
            pool.tensor_scalar(a, k.s_c[:, 0:1], 1.0, None, ALU.min).then_inc(self.own.sem, 1)
            pool.wait_ge(*self.own.next())
            tt(b, a, k.c_mhalf, ALU.pow)
            tt(b, b, b, ALU.mult, 0, s["kv_scale"])
        for j, kind in enumerate(self.pre):
            pool.wait_ge(*s["w_lo"].by(j - 1))
            self.scales(pool, kind, j, 0, j + 1)

    def pool(self, pool):
        k, s = self.k, self.s

        def tt(*args):
            self.tt(pool, *args)

        pool.wait_ge(*self.before.by(self.before_count))
        if not self.ahead:
            self.pool_ahead(pool)
        pool.wait_ge(*s["stat"].by(1))
        if self.layer == 3:
            tt(k.rstd[:, :], k.var[:, :], k.c_mhalf.broadcast_to([P, 8]), ALU.pow)
            tt(k.rstd[:, :], k.rstd[:, :], k.joint[:, 0:1].broadcast_to([P, 8]), ALU.mult, 0, s["rstd"])
        else:
            tt(k.rstd[:, :], k.var[:, :], k.c_mhalf.broadcast_to([P, 8]), ALU.pow, 0, s["rstd"])
        if self.layer == 2:
            pool.wait_ge(*s["masks"].by(17))

        def emit(t, events):
            par = parity(t)
            for e in events:
                if e[0] == "w_sum":
                    _, n, misc = e
                    kind = self.kinds[n]
                    pp = par if kind == "o" else 1 - par
                    pool.wait_ge(*(s["xadd"] if kind == "o" else s["top"]).by(at(t, 8, -7 if kind == "o" else -3 if self.layer == 0 else 0)))
                    if kind != "o" and self.layer == 3:
                        pool.wait_ge(*s["exped"].by(at(t, 8, 0)))
                    pool.wait_ge(*s["w_lo"].by(at(t, self.NK, self.NP + n - 1)))
                    self.scales(pool, kind, self.NP + n + self.NK * par, pp, at(t, self.misc_per, self.NP + misc + 1), t)
                elif e[0] == "k_rms":
                    part = e[1]
                    pool.wait_ge(*s["k_tot"].by(at(t, 2, part + 1)))
                    pool.wait_ge(*s["k_n"].by(at(t, 2, part)))
                    tt(k.krs[:, :], k.ktot[:, :], k.c_mhalf.broadcast_to([P, 4]), ALU.pow, t, s["k_rs"])
                elif e[0] == "q_turn":
                    _, misc, part = e
                    pool.wait_ge(*s["misc_read"].by(at(t, self.misc_per, self.NP + misc + 1)))
                    pool.wait_ge(*s["biased"].by(at(t, 8, 4 * part - 4)))
                    tt(k.rq[:, part, :], k.qtot2[:, :], k.c_mhalf.broadcast_to([P, 16]), ALU.pow, t)
                    tt(k.rq[:, part, :], k.rq[:, part, :], k.kscale[:, 0:1].broadcast_to([P, 16]), ALU.mult, t, s["q_rs"])
                elif e[0] == "scores" and self.layer == 2:
                    b = e[1]
                    i2, pair = b % 2, b % 8
                    pool.wait_ge(*(s["bias0"], s["bias1"])[i2].by(at(t, 64, 16 * (b // 2 + 1))))
                    bias = k.bias_in[:, i2, :].rearrange("p (h n) -> p h n", h=HG)
                    mask = k.mask2[:, pair:pair + 1, :].broadcast_to([P, HG, S])
                    tt(bias, bias, mask, ALU.add, t, s["bias_sum"])
                elif e[0] == "rinv":
                    b = e[1]
                    pool.wait_ge(*s["rinv"].by(at(t, 8, b + 1)))
                    E = k.E[:, b % 2, :].rearrange("p (h n) -> p h n", h=HG)
                    r = k.rinv[:, b % 2, :].rearrange("p (h o) -> p h o", o=1).broadcast_to([P, HG, P])
                    tt(E, E, r, ALU.mult, t, s["probs"])

        self.periods(pool, emit, self.own, self.CHAIN["pool"][self.layer])


class Front:

    NAMES = ["stat", "rstd", "xn", "xt", "xt_s", "dve", "pool", "act", "w", "x"]

    def __init__(self, k, name, names, before, before_count, dram):
        self.k, self.dram, self.before, self.before_count = k, dram, before, before_count
        self.follower = None
        totals = {"stat": 1, "rstd": 1, "xn": TILES, "xt": TILES, "xt_s": TILES, "x": TILES, "xb": TILES}
        self.s = k.signals(name, self.NAMES + names, totals)

    def begin(self, eng):
        eng.wait_ge(*self.before.by(self.before_count))

    def pool_front(self, pool):
        k, s = self.k, self.s
        pool.wait_ge(*s["stat"].by(1))
        pool.tensor_tensor(k.rstd[:, :], k.var[:, :], k.c_mhalf.broadcast_to([P, 8]), ALU.pow).then_inc(s["rstd"].sem, 1)

    def dve_front(self, dve, ch):
        k, s = self.k, self.s
        k.ln_stats(dve, ch, s)
        dve.wait_ge(*s["rstd"].by(1))
        for t in range(TILES):
            dve.tensor_scalar(k.xn[:, t, :], k.x[:, t, :], k.mv[:, t, 0:1], k.rstd[:, t:t + 1],
                              ALU.subtract, ALU.mult).then_inc(s["xn"].sem, 1)

    def pe_front(self, pe):
        k, s = self.k, self.s
        for t in range(TILES):
            pe.wait_ge(*s["xn"].by(t + 1))
            pe.wait_ge(*s["xt_s"].by(t - 1))
            for c in range(KC):
                ins = pe.transpose(k.bank[t % 2][:, c * P:(c + 1) * P], k.xn[:, t, c * P:(c + 1) * P], k.ident[:, :])
            ins.then_inc(s["xt"].sem, 1)

    def act_front(self, act):
        k, s = self.k, self.s
        for t in range(TILES):
            act.wait_ge(*s["xt"].by(t + 1))
            act.activation(k.xtf[:, :, t * P:(t + 1) * P],
                           k.bank[t % 2][:, :].rearrange("p (c n) -> p c n", c=KC), ACT.Copy).then_inc(s["xt_s"].sem, 1)

    def pool_bias(self, pool, bias):
        k, s = self.k, self.s
        for t in range(TILES):
            pool.wait_ge(*s["xn"].by(t + 1))
            pool.tensor_tensor(k.x[:, t, :], k.x[:, t, :], bias, ALU.add).then_inc(s["xb"].sem, 1)


def bc(col, n):
    return col.rearrange("p (m o) -> p m o", o=1).broadcast_to([col.shape[0], col.shape[-1], n])


class BinaryFFN(Front):

    def __init__(self, k, before, count, dram):
        super().__init__(k, "f0", ["xb", "sign", "lg", "top", "ex", "route", "rt", "rt_s", "insc",
                                   "outsc", "out_s", "y", "yt", "yt_s", "main"], before, count, dram)
        v = k.view
        self.w, self.lt = v(8192, [KC, D]), v(15232, [KC, D])
        self.gate = v(10240, [KC, E8])
        self.ics, self.ocs = v(10304, [D])[0:E8], v(10816, [D])[0:E8]
        self.bias = v(11328, [D])
        self.rt = v(11840, [TOK])[0:E8]
        self.z, self.e, self.nm, self.sm = v(12864, [64]), v(12928, [64]), v(12992, [8]), v(13000, [8])
        self.yt = v(13184, [2, D])
        self.osc = v(14208, [2, D])

    def sp(self, sp):
        self.begin(sp)
        d, s = self.dram, self.s
        for dst, src in ((self.w[:, :, :], d["w"]), (self.gate[:, :, :], d["gate"]), (self.ics, d["ics"]),
                         (self.ocs, d["ocs"]), (self.bias[:, :], d["bias"].partition_broadcast(P))):
            sp.dma_start(dst, src).then_inc(s["w"].sem, 16)

    def pool(self, pool):
        self.begin(pool)
        self.pool_front(pool)
        pool.wait_ge(*self.s["w"].by(80))
        self.pool_bias(pool, self.bias[:, :])

    def act(self, act):
        k, s, bank = self.k, self.s, self.k.bank
        self.begin(act)
        self.act_front(act)
        act.wait_ge(*s["top"].by(1))
        act.activation(self.e[:, :], self.z[:, :], ACT.Exp).then_inc(s["ex"].sem, 1)
        for h in range(2):
            act.wait_ge(*s["rt"].by(1))
            act.activation(self.rt[:, h * 512:(h + 1) * 512], bank[3 + h][0:E8, :], ACT.Copy).then_inc(s["rt_s"].sem, 1)
        for i in range(TILES + 1):
            if i < TILES:
                act.wait_ge(*s["outsc"].by(i + 1))
                act.wait_ge(*s["x"].by(i - 1))
                act.activation(self.osc[:, i % 2, :], bank[6][:, :], ACT.Copy).then_inc(s["out_s"].sem, 1)
            if i >= 1:
                act.wait_ge(*s["yt"].by(i))
                act.wait_ge(*s["main"].by(i - 2))
                act.activation(self.yt[:, (i - 1) % 2, :], bank[(i - 1) % 2][:, :], ACT.Copy).then_inc(s["yt_s"].sem, 1)

    def dve(self, dve):
        k, s, bank = self.k, self.s, self.k.bank
        self.begin(dve)
        ch = Chain(s["dve"])
        self.dve_front(dve, ch)
        dve.wait_ge(*s["w"].by(80))
        dve.tensor_scalar(self.lt[:, :, :], self.w[:, :, :], 0.0, None, ALU.is_lt).then_inc(ch.sem, 1)
        dve.wait_ge(*ch.next())
        dve.scalar_tensor_tensor(out=self.w[:, :, :], in0=self.w[:, :, :], scalar=0.0, in1=self.lt[:, :, :],
                                 op0=ALU.is_gt, op1=ALU.subtract).then_inc(s["sign"].sem, 1)
        k.softmax8(dve, ch, s, bank[2][:, 0:64].rearrange("p (t e) -> p t e", e=E8), self)
        e3 = self.e[:, :].rearrange("p (t e) -> p t e", e=E8)
        dve.tensor_tensor(e3, e3, bc(self.sm[:, :], E8), ALU.mult).then_inc(s["route"].sem, 1)
        for i in range(TILES + 2):
            if i < TILES:
                dve.wait_ge(*s["insc"].by(i + 1))
                dve.tensor_tensor(k.xn[:, i, :], k.xn[:, i, :], bank[5][:, :], ALU.mult).then_inc(s["y"].sem, 1)
            if i >= 2:
                j = i - 2
                dve.wait_ge(*s["main"].by(j + 1))
                dve.wait_ge(*s["out_s"].by(j + 1))
                dve.tensor_tensor(self.osc[:, j % 2, :], bank[7][:, :], self.osc[:, j % 2, :], ALU.mult).then_inc(ch.sem, 1)
                dve.wait_ge(*ch.next())
                dve.wait_ge(*s["xb"].by(j + 1))
                dve.tensor_tensor(k.x[:, j, :], k.x[:, j, :], self.osc[:, j % 2, :], ALU.add).then_inc(s["x"].sem, 1)

    def pe(self, pe):
        k, s, bank = self.k, self.s, self.k.bank
        self.begin(pe)
        self.pe_front(pe)
        pe.wait_ge(*s["w"].by(80))
        for t in range(TILES):
            pe.wait_ge(*s["xt_s"].by(t + 1))
            for c in range(KC):
                ins = pe.matmul(bank[2][:, t * E8:(t + 1) * E8], k.xtf[:, c, t * P:(t + 1) * P], self.gate[:, c, :],
                                start=c == 0, stop=c == KC - 1)
        ins.then_inc(s["lg"].sem, 1)
        pe.wait_ge(*s["route"].by(1))
        for t in range(TILES):
            ins = pe.transpose(bank[3 + t // 4][0:E8, (t % 4) * P:(t % 4 + 1) * P],
                               self.e[:, t * E8:(t + 1) * E8], k.ident[:, :])
        ins.then_inc(s["rt"].sem, 1)
        pe.wait_ge(*s["rt_s"].by(2))
        pe.wait_ge(*s["sign"].by(1))
        for i in range(TILES + 2):
            if i < TILES:
                pe.wait_ge(*s["y"].by(i))
                pe.matmul(bank[5][:, :], self.rt[:, i * P:(i + 1) * P], self.ics, start=True, stop=True).then_inc(s["insc"].sem, 1)
                pe.wait_ge(*s["out_s"].by(i))
                pe.matmul(bank[6][:, :], self.rt[:, i * P:(i + 1) * P], self.ocs, start=True, stop=True).then_inc(s["outsc"].sem, 1)
            if 0 <= i - 1 < TILES:
                j = i - 1
                pe.wait_ge(*s["y"].by(j + 1))
                pe.wait_ge(*s["yt_s"].by(j - 1))
                for c in range(KC):
                    ins = pe.transpose(bank[j % 2][:, c * P:(c + 1) * P], k.xn[:, j, c * P:(c + 1) * P], k.ident[:, :])
                ins.then_inc(s["yt"].sem, 1)
            if i >= 2:
                j = i - 2
                pe.wait_ge(*s["yt_s"].by(j + 1))
                pe.wait_ge(*s["x"].by(j))
                for c in range(KC):
                    ins = pe.matmul(bank[7][:, :], self.yt[:, j % 2, c * P:(c + 1) * P], self.w[:, c, :],
                                    start=c == 0, stop=c == KC - 1)
                ins.then_inc(s["main"].sem, 1)


class NarrowAttention(Front):

    def __init__(self, k, before, count, dram):
        super().__init__(k, "x1", ["proj", "proj_s", "scores", "biased", "top", "ex", "rinv", "probs",
                                   "turned", "pt", "mixed"], before, count, dram)
        v = k.view
        self.Q, self.K, self.ctx_t = v(8192, [KC, TOK]), v(12288, [KC, TOK]), v(16384, [KC, TOK])
        self.wq, self.wk = v(20480, [KC, D]), v(22528, [KC, D])
        self.ctx = k.wo_f.rearrange("p (t n) -> p t n", t=TILES)
        self.b = k.small

    def sp(self, sp):
        self.begin(sp)
        d, s = self.dram, self.s
        for dst, src in ((self.ctx_t[:, :, :], d["ctx_t"]), (self.wk[:, :, :], d["wk"]), (self.b[:, 0:4], d["bk"]),
                         (self.wq[:, :, :], d["wq"]), (self.b[:, 4:8], d["bq"]), (self.ctx, d["ctx"])):
            sp.dma_start(dst, src).then_inc(s["w"].sem, 16)

    def pool(self, pool):
        k, s = self.k, self.s
        self.begin(pool)
        self.pool_front(pool)
        for j in range(2):
            pool.wait_ge(*s["rinv"].by(j + 1))
            E = k.E[:, j, :].rearrange("p (h n) -> p h n", h=HG)
            pool.tensor_tensor(E, E, bc(k.rinv[:, j, :], P), ALU.mult).then_inc(s["probs"].sem, 1)

    def act(self, act):
        k, s, bank = self.k, self.s, self.k.bank
        self.begin(act)

        def evac(m):
            dst, col = (self.K, 0) if m < 8 else (self.Q, 4)
            dc, hf = (m % 8) // 2, m % 2
            act.wait_ge(*s["proj"].by(m + 1))
            act.activation(dst[:, dc, hf * 512:(hf + 1) * 512], bank[2 + m % 2][:, :], ACT.Identity,
                           bias=self.b[:, col + dc:col + dc + 1]).then_inc(s["proj_s"].sem, 1)

        for m in range(8):
            evac(m)
        self.act_front(act)
        for m in range(8, 16):
            evac(m)
        for j in range(2):
            act.wait_ge(*s["top"].by(j + 1))
            for h in range(4):
                cols = slice(h * P, (h + 1) * P)
                ins = act.activation(k.E[:, j, cols], k.Sm[:, j, cols], ACT.Exp, bias=k.nmax[:, j, h:h + 1],
                                     accum_out=k.rsum[:, j, h:h + 1])
            ins.then_inc(s["ex"].sem, 1)
        for j in range(2):
            act.wait_ge(*s["turned"].by(j + 1))
            act.activation(k.Sm[:, j, :], bank[6 + j][:, :], ACT.Copy).then_inc(s["pt"].sem, 1)

    def dve(self, dve):
        k, s, bank = self.k, self.s, self.k.bank
        self.begin(dve)
        ch = Chain(s["dve"])
        self.dve_front(dve, ch)
        for j in range(2):
            dve.wait_ge(*s["scores"].by(j + 1))
            Sm = k.Sm[:, j, :].rearrange("p (h n) -> p h n", h=HG)
            dve.scalar_tensor_tensor(out=Sm, in0=bank[4 + j][:, :].rearrange("p (h n) -> p h n", h=HG),
                                     scalar=1.0 / math.sqrt(D),
                                     in1=k.blocks[:, :].rearrange("p (o n) -> p o n", o=1).broadcast_to([P, HG, P]),
                                     op0=ALU.mult, op1=ALU.add).then_inc(ch.sem, 1)
            dve.wait_ge(*ch.next())
            dve.tensor_reduce(k.nmax[:, j, :], Sm, AX.X, ALU.max, negate=True).then_inc(s["top"].sem, 1)
        for j in range(2):
            dve.wait_ge(*s["ex"].by(j + 1))
            dve.reciprocal(k.rinv[:, j, :], k.rsum[:, j, :]).then_inc(s["rinv"].sem, 1)
        for t in range(TILES):
            dve.wait_ge(*s["mixed"].by(t + 1))
            dve.tensor_tensor(k.x[:, t, :], k.x[:, t, :], bank[t % 2][:, :], ALU.add).then_inc(s["x"].sem, 1)

    def pe(self, pe):
        k, s, bank = self.k, self.s, self.k.bank
        self.begin(pe)
        pe.wait_ge(*s["w"].by(96))

        def project(m):
            w, src = (self.wk, self.ctx_t) if m < 8 else (self.wq, k.xtf)
            dc, hf = (m % 8) // 2, m % 2
            pe.wait_ge(*s["proj_s"].by(m - 1))
            for c in range(KC):
                ins = pe.matmul(bank[2 + m % 2][:, :], w[:, c, dc * P:(dc + 1) * P], src[:, c, hf * 512:(hf + 1) * 512],
                                start=c == 0, stop=c == KC - 1)
            ins.then_inc(s["proj"].sem, 1)

        for m in range(8):
            project(m)
        self.pe_front(pe)
        pe.wait_ge(*s["xt_s"].by(TILES))
        for m in range(8, 16):
            project(m)
        pe.wait_ge(*s["proj_s"].by(16))
        for j in range(2):
            for h in range(4):
                lo = (j * 4 + h) * P
                for c in range(KC):
                    ins = pe.matmul(bank[4 + j][:, h * P:(h + 1) * P], self.Q[:, c, lo:lo + P], self.K[:, c, lo:lo + P],
                                    start=c == 0, stop=c == KC - 1)
            ins.then_inc(s["scores"].sem, 1)
        for j in range(2):
            pe.wait_ge(*s["probs"].by(j + 1))
            for h in range(4):
                ins = pe.transpose(bank[6 + j][:, h * P:(h + 1) * P], k.E[:, j, h * P:(h + 1) * P], k.ident[:, :])
            ins.then_inc(s["turned"].sem, 1)
        for t in range(TILES):
            pe.wait_ge(*s["pt"].by(t // 4 + 1))
            pe.wait_ge(*s["x"].by(t - 1))
            pe.matmul(bank[t % 2][:, :], k.Sm[:, t // 4, (t % 4) * P:(t % 4 + 1) * P], self.ctx[:, t, :],
                      start=True, stop=True).then_inc(s["mixed"].sem, 1)


class FourierFFN(Front):

    def __init__(self, k, before, count, dram):
        super().__init__(k, "f1", ["masked", "ws", "g", "g_s", "et", "et_s", "one", "main"], before, count, dram)
        v = k.view
        self.w, self.f = v(8192, [KC, D]), v(10240, [KC, D])
        self.enc = v(14336, [KC, R40])
        self.co = v(14496, [KC, 3, R40])
        self.mask = v(14976, [120]).bitcast(U8).rearrange("p (c e r) -> p c e r", c=KC, e=3)
        self.ws = v(15136, [KC, R40])
        self.g = v(19456, [D])[0:R40 + 1]
        self.et = v(18432, [TOK])[0:R40 + 1]

    def sp(self, sp):
        self.begin(sp)
        d, s = self.dram, self.s
        for dst, src in ((self.co[:, :, :, :], d["co"]), (self.mask, d["mask"]), (self.f[:, :, :], d["f"]),
                         (self.enc[:, :, :], d["enc"]), (self.w[:, :, :], d["w"]),
                         (self.g[R40:R40 + 1, :], d["bias"])):
            sp.dma_start(dst, src).then_inc(s["w"].sem, 16)
        self.follower.sp_ahead(sp)

    def pool(self, pool):
        self.begin(pool)
        pool.memset(self.et[:, :], 1.0).then_inc(self.s["one"].sem, 1)
        self.pool_front(pool)
        self.follower.pool_ahead(pool)

    def act(self, act):
        k, s, bank = self.k, self.s, self.k.bank
        self.begin(act)
        act.wait_ge(*s["g"].by(1))
        act.activation(self.g[0:R40, :], bank[2][0:R40, :], ACT.Copy, scale=0.5).then_inc(s["g_s"].sem, 1)
        self.act_front(act)
        act.wait_ge(*s["one"].by(1))
        for h in range(2):
            act.wait_ge(*s["et"].by(h + 1))
            act.activation(self.et[0:R40, h * 512:(h + 1) * 512], bank[3 + h][0:R40, :], ACT.Copy).then_inc(s["et_s"].sem, 1)
        self.follower.act_ahead(act)

    def dve(self, dve):
        k, s, bank = self.k, self.s, self.k.bank
        self.begin(dve)
        ch = Chain(s["dve"])
        dve.wait_ge(*s["w"].by(96))
        dve.tensor_tensor(self.co[:, :, :, :], self.co[:, :, :, :], self.mask, ALU.mult).then_inc(ch.sem, 1)
        dve.wait_ge(*ch.next())
        dve.tensor_tensor(self.ws[:, :, :], self.co[:, :, 0, :], self.co[:, :, 1, :], ALU.add).then_inc(ch.sem, 1)
        dve.wait_ge(*ch.next())
        dve.tensor_tensor(self.ws[:, :, :], self.ws[:, :, :], self.co[:, :, 2, :], ALU.add).then_inc(s["ws"].sem, 1)
        self.dve_front(dve, ch)
        for t in range(TILES):
            dve.wait_ge(*s["main"].by(t + 1))
            dve.tensor_tensor(k.x[:, t, :], k.x[:, t, :], bank[5 + t % 2][:, :], ALU.add).then_inc(s["x"].sem, 1)
            if self.follower and t // 2 < self.follower.NP:
                if t % 2 == 0:
                    self.follower.total_ahead(dve, t // 2)
                else:
                    self.follower.low_ahead(dve, t // 2)

    def pe(self, pe):
        k, s, bank = self.k, self.s, self.k.bank
        self.begin(pe)
        pe.wait_ge(*s["w"].by(96))
        pe.wait_ge(*s["ws"].by(1))
        for c in range(KC):
            ins = pe.matmul(bank[2][0:R40, :], self.ws[:, c, :], self.f[:, c, :], start=c == 0, stop=c == KC - 1)
        ins.then_inc(s["g"].sem, 1)
        self.pe_front(pe)
        for h in range(2):
            pe.wait_ge(*s["xt_s"].by(4 * h + 4))
            for c in range(KC):
                ins = pe.matmul(bank[3 + h][0:R40, :], self.enc[:, c, :], k.xtf[:, c, h * 512:(h + 1) * 512],
                                start=c == 0, stop=c == KC - 1)
            ins.then_inc(s["et"].sem, 1)
        pe.wait_ge(*s["g_s"].by(1))
        for t in range(TILES):
            pe.wait_ge(*s["x"].by(t - 1))
            pe.wait_ge(*s["et_s"].by(t // 4 + 1))
            out = bank[5 + t % 2][:, :]
            for c in range(KC):
                pe.matmul(out, k.xtf[:, c, t * P:(t + 1) * P], self.w[:, c, :], start=c == 0, stop=False)
            pe.matmul(out, self.et[:, t * P:(t + 1) * P], self.g, start=False, stop=True).then_inc(s["main"].sem, 1)
            if self.follower and t % 2 == 0 and t // 2 < self.follower.NP:
                self.follower.sum_ahead(pe, t // 2)


class AdapterFFN(Front):

    def __init__(self, k, layer, before, count, dram):
        super().__init__(k, f"f{layer}", ["xb", "lg", "top", "ex", "iota", "h", "hw", "ht", "ht_s", "main", "out"],
                         before, count, dram)
        self.layer, self.G = layer, 9 if layer == 2 else 8
        v = k.view
        self.w = v(8192, [KC, D])
        self.gate = v(10240, [KC, self.G])
        self.a = v(10304, [KC, P])
        self.bm = v(10816, [D])
        self.bias = v(11328, [D])
        self.hw = v(18432, [TILES, P])
        self.ht = v(16384, [2, P])
        cols = iter(range(16640, 18400, 80))
        self.z9, self.e9, self.z, self.e, self.g2, self.m8, self.oh = (v(next(cols), [72]) for _ in range(7))
        self.idx, self.idf = v(next(cols), [64]), v(next(cols), [64])
        self.nm, self.sm, self.thr, self.p1, self.p2 = (v(next(cols), [8]) for _ in range(5))
        self.bthr, self.iota = v(next(cols), [1]), v(next(cols), [8])

    def sp(self, sp):
        self.begin(sp)
        d, s = self.dram, self.s
        loads = [(self.gate[:, :, :], d["gate"]), (self.a[:, :, :], d["a"]), (self.w[:, :, :], d["w"]),
                 (self.bm[:, :], d["bm"]), (self.bias[:, :], d["bias"].partition_broadcast(P))]
        if self.layer == 2:
            loads.append((self.bthr[:, :], d["bthr"].partition_broadcast(P)))
        for dst, src in loads:
            sp.dma_start(dst, src).then_inc(s["w"].sem, 16)
        if self.follower:
            self.follower.sp_ahead(sp)
        self.loads = 16 * len(loads)
        if self.layer == 3:
            for t in range(TILES):
                sp.wait_ge(*s["x"].by(t + 1))
                sp.dma_start(d["out"][t * P:(t + 1) * P, :], self.k.x[:, t, :]).then_inc(s["out"].sem, 16)
            sp.wait_ge(*s["out"].by(16 * TILES))

    def all_loads(self):
        return 96 if self.layer == 2 else 80

    def pool(self, pool):
        k, s = self.k, self.s
        self.begin(pool)
        if self.layer == 3:
            for e in range(E8):
                ins = pool.memset(self.iota[:, e:e + 1], float(e))
            ins.then_inc(s["iota"].sem, 1)
        self.pool_front(pool)
        pool.wait_ge(*s["w"].by(self.all_loads()))
        self.pool_bias(pool, self.bias[:, :])
        if self.follower:
            self.follower.pool_ahead(pool)

    def act(self, act):
        k, s, bank = self.k, self.s, self.k.bank
        self.begin(act)
        self.act_front(act)
        act.wait_ge(*s["top"].by(1))
        if self.layer == 2:
            act.activation(self.e[:, 0:64], self.z[:, 0:64], ACT.Exp).then_inc(s["ex"].sem, 1)
            act.activation(self.e9[:, 0:8], self.z9[:, 0:8], ACT.Exp).then_inc(s["ex"].sem, 1)
        else:
            act.activation(self.e[:, 0:8], self.z[:, 0:8], ACT.Exp).then_inc(s["ex"].sem, 2)
        for t in range(TILES):
            if self.follower and t % 2 == 0 and t // 2 < self.follower.NP:
                self.follower.squares_ahead(act, t // 2)
            act.wait_ge(*s["ht"].by(t + 1))
            act.wait_ge(*s["main"].by(t - 1))
            act.activation(self.ht[:, t % 2, :], bank[t % 2][:, 0:P], ACT.Copy).then_inc(s["ht_s"].sem, 1)
            if self.follower and t % 2 and t // 2 < self.follower.NP:
                self.follower.high_ahead(act, t // 2)

    def gates2(self, dve, ch):
        k, s = self.k, self.s
        lg = k.bank[2][:, 0:72].rearrange("p (t e) -> p t e", e=9)
        col = lg[:, :, 8:9].rearrange("p t o -> p (t o)")
        z9, thr = self.z9[:, 0:8], self.thr[:, :]
        dve.wait_ge(*s["lg"].by(1))
        dve.tensor_scalar(z9, col, self.bthr[:, 0:1], -1.0, ALU.add, ALU.mult).then_inc(ch.sem, 1)
        dve.wait_ge(*ch.next())
        k.softmax8(dve, ch, s, lg[:, :, 0:8], self)
        dve.wait_ge(*s["ex"].by(2))
        dve.tensor_scalar(self.p1[:, :], self.e9[:, 0:8], 1.0, None, ALU.add).then_inc(ch.sem, 1)
        dve.wait_ge(*ch.next())
        dve.reciprocal(self.p2[:, :], self.p1[:, :]).then_inc(ch.sem, 1)
        dve.wait_ge(*ch.next())
        dve.tensor_scalar(thr, self.p2[:, :], 0.125, None, ALU.mult).then_inc(ch.sem, 1)
        dve.wait_ge(*ch.next())
        e3 = self.e[:, 0:64].rearrange("p (t e) -> p t e", e=8)
        dve.tensor_tensor(e3, e3, bc(self.sm[:, :], 8), ALU.mult).then_inc(ch.sem, 1)
        dve.wait_ge(*ch.next())
        dve.tensor_tensor(e3, e3, bc(thr, 8), ALU.subtract).then_inc(ch.sem, 1)
        dve.wait_ge(*ch.next())
        dve.tensor_scalar(self.e[:, 0:64], self.e[:, 0:64], 0.0, None, ALU.max).then_inc(ch.sem, 1)
        dve.wait_ge(*ch.next())
        dve.tensor_reduce(self.nm[:, :], e3, AX.X, ALU.add).then_inc(ch.sem, 1)
        dve.wait_ge(*ch.next())
        dve.scalar_tensor_tensor(out=self.p1[:, :], in0=self.nm[:, :], scalar=0.0, in1=self.nm[:, :],
                                 op0=ALU.is_equal, op1=ALU.add).then_inc(ch.sem, 1)
        dve.wait_ge(*ch.next())
        dve.reciprocal(self.p2[:, :], self.p1[:, :]).then_inc(ch.sem, 1)
        dve.wait_ge(*ch.next())
        dve.tensor_scalar(self.p2[:, :], self.p2[:, :], 2.0, None, ALU.mult).then_inc(ch.sem, 1)
        dve.wait_ge(*ch.next())
        g3 = self.g2[:, 0:64].rearrange("p (t e) -> p t e", e=8)
        dve.tensor_tensor(g3, e3, bc(self.p2[:, :], 8), ALU.mult).then_inc(ch.sem, 1)
        dve.wait_ge(*ch.next())

    def gates3(self, dve, ch):
        k, s = self.k, self.s
        m3 = self.m8[:, 0:64].rearrange("p (t e) -> p t e", e=8)
        i3 = self.idx[:, 0:64].bitcast(U32).rearrange("p (t e) -> p t e", e=8)
        dve.wait_ge(*s["lg"].by(1))
        dve.tensor_copy(self.z9[:, 0:64], k.bank[2][:, 0:64]).then_inc(ch.sem, 1)
        dve.wait_ge(*ch.next())
        for t in range(TILES):
            ins = dve.max(self.m8[:, t * 8:t * 8 + 8], self.z9[:, t * 8:t * 8 + 8])
        ins.then_inc(ch.sem, 1)
        dve.wait_ge(*ch.next())
        for t in range(TILES):
            ins = dve.max_index(i3[:, t, :], self.m8[:, t * 8:t * 8 + 8], self.z9[:, t * 8:t * 8 + 8])
        ins.then_inc(ch.sem, 1)
        dve.wait_ge(*ch.next())
        col = lambda v, i: v[:, :, i:i + 1].rearrange("p t o -> p (t o)")
        dve.tensor_tensor(self.z[:, 0:8], col(m3, 1), col(m3, 0), ALU.subtract).then_inc(s["top"].sem, 1)
        f3 = self.idf[:, :].rearrange("p (t e) -> p t e", e=8)
        dve.tensor_copy(f3, i3).then_inc(ch.sem, 1)
        dve.wait_ge(*ch.next())
        dve.wait_ge(*s["ex"].by(2))
        dve.tensor_scalar(self.nm[:, :], self.e[:, 0:8], 1.0, None, ALU.add).then_inc(ch.sem, 1)
        dve.wait_ge(*ch.next())
        dve.reciprocal(self.sm[:, :], self.nm[:, :]).then_inc(ch.sem, 1)
        dve.wait_ge(*ch.next())
        dve.tensor_scalar(self.p1[:, :], self.sm[:, :], 2.0, None, ALU.mult).then_inc(ch.sem, 1)
        dve.wait_ge(*ch.next())
        dve.tensor_tensor(self.p2[:, :], self.p1[:, :], self.e[:, 0:8], ALU.mult).then_inc(ch.sem, 1)
        dve.wait_ge(*ch.next())
        dve.wait_ge(*s["iota"].by(1))
        io = self.iota[:, :].rearrange("p (o e) -> p o e", o=1).broadcast_to([P, 8, 8])
        g3 = self.g2[:, 0:64].rearrange("p (t e) -> p t e", e=8)
        o3 = self.oh[:, 0:64].rearrange("p (t e) -> p t e", e=8)
        dve.tensor_tensor(g3, io, f3[:, :, 0:1].broadcast_to([P, 8, 8]), ALU.is_equal).then_inc(ch.sem, 1)
        dve.wait_ge(*ch.next())
        dve.tensor_tensor(o3, io, f3[:, :, 1:2].broadcast_to([P, 8, 8]), ALU.is_equal).then_inc(ch.sem, 1)
        dve.wait_ge(*ch.next())
        dve.tensor_tensor(g3, g3, bc(self.p1[:, :], 8), ALU.mult).then_inc(ch.sem, 1)
        dve.wait_ge(*ch.next())
        dve.tensor_tensor(o3, o3, bc(self.p2[:, :], 8), ALU.mult).then_inc(ch.sem, 1)
        dve.wait_ge(*ch.next())
        dve.tensor_tensor(g3, g3, o3, ALU.add).then_inc(ch.sem, 1)
        dve.wait_ge(*ch.next())

    def dve(self, dve):
        k, s, bank = self.k, self.s, self.k.bank
        self.begin(dve)
        ch = Chain(s["dve"])
        self.dve_front(dve, ch)
        dve.wait_ge(*s["w"].by(self.all_loads()))
        (self.gates2 if self.layer == 2 else self.gates3)(dve, ch)
        for q in range(2):
            dve.wait_ge(*s["h"].by(q + 1))
            g = self.g2[:, q * 32:q * 32 + 32]
            dve.tensor_tensor(self.hw[:, q * 4:q * 4 + 4, :].rearrange("p t (e r) -> p (t e) r", e=E8),
                              bank[3 + q][:, :].rearrange("p (m r) -> p m r", r=R16), bc(g, R16), ALU.mult)\
               .then_inc(s["hw"].sem, 1)
        for t in range(TILES):
            dve.wait_ge(*s["main"].by(t + 1))
            dve.wait_ge(*s["xb"].by(t + 1))
            dve.tensor_tensor(k.x[:, t, :], k.x[:, t, :], bank[5 + t % 2][:, :], ALU.add).then_inc(s["x"].sem, 1)
            if self.follower and t // 2 < self.follower.NP:
                if t % 2 == 0:
                    self.follower.total_ahead(dve, t // 2)
                else:
                    self.follower.low_ahead(dve, t // 2)

    def pe(self, pe):
        k, s, bank = self.k, self.s, self.k.bank
        self.begin(pe)
        self.pe_front(pe)
        pe.wait_ge(*s["w"].by(self.all_loads()))
        G = self.G
        for t in range(TILES):
            pe.wait_ge(*s["xt_s"].by(t + 1))
            for c in range(KC):
                ins = pe.matmul(bank[2][:, t * G:(t + 1) * G], k.xtf[:, c, t * P:(t + 1) * P], self.gate[:, c, :],
                                start=c == 0, stop=c == KC - 1)
        ins.then_inc(s["lg"].sem, 1)
        for t in range(TILES):
            for c in range(KC):
                ins = pe.matmul(bank[3 + t // 4][:, (t % 4) * P:(t % 4 + 1) * P], k.xtf[:, c, t * P:(t + 1) * P],
                                self.a[:, c, :], start=c == 0, stop=c == KC - 1)
            if t % 4 == 3:
                ins.then_inc(s["h"].sem, 1)

        def turn(t):
            pe.wait_ge(*s["hw"].by(t // 4 + 1))
            pe.wait_ge(*s["ht_s"].by(t - 1))
            pe.transpose(bank[t % 2][:, 0:P], self.hw[:, t, :], k.ident[:, :]).then_inc(s["ht"].sem, 1)

        for t in range(TILES):
            out = bank[5 + t % 2][:, :]
            pe.wait_ge(*s["x"].by(t - 1))
            for c in range(KC):
                pe.matmul(out, k.xtf[:, c, t * P:(t + 1) * P], self.w[:, c, :], start=c == 0, stop=False)
            turn(t)
            pe.wait_ge(*s["ht_s"].by(t + 1))
            pe.matmul(out, self.ht[:, t % 2, :], self.bm[:, :], start=False, stop=True).then_inc(s["main"].sem, 1)
            if self.follower and t % 2 == 0 and t // 2 < self.follower.NP:
                self.follower.sum_ahead(pe, t // 2)


class Setup:

    def __init__(self, k, dram):
        self.k, self.dram = k, dram
        names = ["x", "ctx", "ctx_t", "norms", "mask", "fill", "rows", "peak", "factor", "c_hi", "c_lo",
                 "wq", "wmax", "wfac", "pool", "act", "dve", "done"]
        self.s = k.signals("s", names, {})
        self.ctx, self.ctx_t = k.view(4096, [TILES, D]), k.view(0, [KC, TOK])

    def sp(self, sp):
        k, s, d = self.k, self.s, self.dram
        sp.dma_start(self.ctx[:, :, :], d["ctx"]).then_inc(s["ctx"].sem, 16)
        sp.dma_start(k.x[:, :, :], d["x"]).then_inc(s["x"].sem, 16)
        sp.dma_start(self.ctx_t[:, :, :], d["ctx_t"]).then_inc(s["ctx_t"].sem, 16)
        sp.dma_start(k.small[:, 8:9], d["qn"]).then_inc(s["norms"].sem, 16)
        sp.dma_start(k.small[:, 9:10], d["kn"]).then_inc(s["norms"].sem, 16)
        sp.wait_ge(*s["fill"].by(3))
        for q in range(2):
            rows = slice(q * S, (q + 1) * S)
            sp.dma_start(k.mask0[rows, rows], d["mask"]).then_inc(s["mask"].sem, 16)

    def act(self, act):
        k, s = self.k, self.s
        act.wait_ge(*s["ctx"].by(16))
        ch = Chain(s["act"])
        for t in range(TILES):
            act.activation(k.Sm[:, 0, :], self.ctx[:, t, :], ACT.Square, accum_out=k.rows[:, t:t + 1]).then_inc(ch.sem, 1)
            act.wait_ge(*ch.next())
        act.wait_ge(*s["factor"].by(1))
        act.wait_ge(*s["ctx_t"].by(16))
        for c in range(KC):
            act.activation(k.ct[:, 0, c, :], self.ctx_t[:, c, :], ACT.Copy, scale=k.s_c[:, 0:1]).then_inc(s["c_hi"].sem, 1)

    def dve(self, dve):
        k, s = self.k, self.s
        dve.memset(k.mask0[:, :], -LARGE).then_inc(s["fill"].sem, 1)
        dve.memset(k.blocks[:, :], -LARGE).then_inc(s["fill"].sem, 1)
        dve.wait_ge(*s["fill"].by(2))
        for q in range(2):
            rows = slice(q * S, (q + 1) * S)
            ins = dve.memset(k.blocks[rows, rows], 0.0)
        ins.then_inc(s["fill"].sem, 1)
        dve.wait_ge(*s["act"].by(TILES))
        dve.tensor_reduce(k.peak[:, 0:1], k.rows[:, :], AX.X, ALU.max).then_inc(s["rows"].sem, 1)
        dve.wait_ge(*s["norms"].by(32))
        ch = Chain(s["dve"])
        dve.tensor_tensor(k.wqk[:, 0:1], k.small[:, 8:9], k.small[:, 9:10], ALU.mult).then_inc(ch.sem, 1)
        dve.wait_ge(*ch.next())
        dve.tensor_tensor(k.peak[:, 2:3], k.wqk[:, 0:1], k.wqk[:, 0:1], ALU.mult).then_inc(s["wq"].sem, 1)
        dve.wait_ge(*s["factor"].by(1))
        for c in range(KC):
            dve.wait_ge(*s["c_hi"].by(c + 1))
            dve.scalar_tensor_tensor(out=k.ct[:, 1, c, :], in0=self.ctx_t[:, c, :], scalar=k.s_c[:, 0:1],
                                     in1=k.ct[:, 0, c, :], op0=ALU.mult, op1=ALU.subtract).then_inc(s["c_lo"].sem, 1)
        dve.wait_ge(*s["c_lo"].by(KC))
        dve.wait_ge(*s["x"].by(16))
        dve.wait_ge(*s["mask"].by(32))
        dve.wait_ge(*s["wfac"].by(1))
        dve.tensor_copy(k.peak[:, 4:5], k.peak[:, 2:3]).then_inc(s["done"].sem, 1)

    def pool(self, pool):
        k, s = self.k, self.s
        ch = Chain(s["pool"])
        pool.memset(k.ones[:, :], 1.0)
        pool.memset(k.select[:, :, :], 0.0).then_inc(ch.sem, 1)
        pool.wait_ge(*ch.next())
        for h in range(HG):
            pool.memset(k.select[:, h, h:h + 1], 1.0)
        for i, v in enumerate((-0.5, 0.5, C_W, 1.0 / C_W, EPS, SCALE, C_X, 1.0 / C_X, C_N, SCALE / C_N, 1e-30)):
            pool.memset(k.consts[:, i:i + 1], v)
        pool.memset(k.ident[:, :], 0.0).then_inc(ch.sem, 1)
        pool.wait_ge(*ch.next())
        pool.affine_select(out=k.ident[:, :], in_=k.ident[:, :], compare_op=ALU.not_equal, fill=1.0,
                           base=0, pattern=[[-1, P]], channel_multiplier=1).then_inc(ch.sem, 1)
        pool.wait_ge(*ch.next())
        
        def tt(o, a, b, op):
            pool.tensor_tensor(o, a, b, op).then_inc(ch.sem, 1)
            pool.wait_ge(*ch.next())

        tiny = k.consts[:, 10:11]
        pool.wait_ge(*s["rows"].by(1))
        pool.partition_all_reduce(k.peak[:, 1:2], k.peak[:, 0:1], P, RMAX).then_inc(ch.sem, 1)
        pool.wait_ge(*ch.next())
        tt(k.peak[:, 1:2], k.peak[:, 1:2], tiny, ALU.add)
        tt(k.s_c[:, 0:1], k.peak[:, 1:2], k.c_mhalf, ALU.pow)
        tt(k.inv_c[:, 0:1], k.peak[:, 1:2], k.c_half, ALU.pow)
        tt(k.inv_c[:, 0:1], k.inv_c[:, 0:1], k.consts[:, 7:8], ALU.mult)
        pool.tensor_tensor(k.s_c[:, 0:1], k.s_c[:, 0:1], k.consts[:, 6:7], ALU.mult).then_inc(s["factor"].sem, 1)
        pool.wait_ge(*s["wq"].by(1))
        pool.partition_all_reduce(k.peak[:, 3:4], k.peak[:, 2:3], P, RMAX).then_inc(ch.sem, 1)
        pool.wait_ge(*ch.next())
        tt(k.peak[:, 3:4], k.peak[:, 3:4], tiny, ALU.add)
        tt(k.small[:, 10:11], k.peak[:, 3:4], k.c_mhalf, ALU.pow)
        tt(k.small[:, 10:11], k.small[:, 10:11], k.consts[:, 8:9], ALU.mult)
        tt(k.wqk[:, 0:1], k.wqk[:, 0:1], k.small[:, 10:11], ALU.mult)
        tt(k.kscale[:, 0:1], k.peak[:, 3:4], k.c_half, ALU.pow)
        pool.tensor_tensor(k.kscale[:, 0:1], k.kscale[:, 0:1], k.consts[:, 9:10], ALU.mult).then_inc(s["wfac"].sem, 1)


class Kernel:

    def __init__(self, nc, ctx):
        self.nc, self.ctx, self.shared = nc, ctx, {}

        def sb(name, shape, dt=FP32):
            return ctx.enter_context(nc.sbuf_tensor("m_" + name, shape, dt))

        self.x = sb("x", [P, TILES, D])
        self.joint_parts = sb("input_parts", [P, 2 * 2 * KC * TOK], FP16)
        self.xt = self.joint_parts[:, 0:2 * KC * TOK].rearrange("p (i c n) -> p i c n", i=2, c=KC)
        self.ct = self.joint_parts[:, 2 * KC * TOK:].rearrange("p (i c n) -> p i c n", i=2, c=KC)
        self.hid = self.joint_parts[:, :].rearrange("p (i c b n) -> p i c b n", i=2, c=KC, b=B)
        self.arena = sb("arena", [P, 24576])
        self.wo_t = sb("wo_t", [P, 4096])
        self.wo_f = self.wo_t[:, :]
        self.wo = self.wo_t[:, :].bitcast(FP16).rearrange("p (g i c n) -> p g i c n", g=2, i=2, c=KC)
        h = lambda lo, n: self.arena[:, lo:lo + n].bitcast(FP16)
        self.Q = h(0, 4096).rearrange("p (i f h n) -> p i f h n", i=2, f=2, h=HG)
        self.q3 = h(0, 4096).rearrange("p (i f g b h n) -> p i f g b h n", i=2, f=2, g=2, b=8, h=2)
        self.K = h(4096, 4096).rearrange("p (i f h n) -> p i f h n", i=2, f=2, h=HG)
        self.V = h(8192, 4096).rearrange("p (i f h n) -> p i f h n", i=2, f=2, h=HG)
        self.wproj = None
        self.kt3 = h(4096, 8192).rearrange("p (i g b n) -> p i g b n", i=2, g=4, b=B)
        self.v3 = h(16384, 8192).rearrange("p (i b g n) -> p i b g n", i=2, b=B, g=4)
        self.wproj = h(12288, 12288).rearrange("p (k g i c n) -> p k g i c n", k=3, g=2, i=2, c=KC)
        self.wsmall = h(16384, 2048).rearrange("p (k g i c n) -> p k g i c n", k=2, g=2, i=2, c=KC)
        self.qsq, self.qrow = self.view(18432, [HG, 512]), self.view(21520, [512])
        self.q_parts = self.arena[:, 22032:24080].bitcast(BF16).rearrange("p (i h n) -> p i h n", i=2, h=HG)
        self.select = sb("select", [P, HG, P], BF16)
        self.ksq, self.kraw = self.view(20480, [512]), self.view(20992, [512])
        self.ksum, self.ktot, self.krs = self.view(21504, [4]), self.view(21508, [4]), self.view(21512, [4])
        self.xn, self.xtf = self.view(0, [TILES, D]), self.view(4096, [KC, TOK])
        self.ctx_in = self.view(0, [KC, TOK])
        self.raw = sb("raw", [P, 2, 2048])
        self.Sm, self.E = sb("Sm", [P, 2, 512]), sb("E", [P, 2, 512])
        self.PT, self.A = sb("PT", [P, 2, 2, 512], FP16), sb("A", [P, 2, 2, 512], FP16)
        self.bias_in = sb("bias_in", [P, 2, 256])
        self.mask_u8, self.mask2 = sb("mask_u8", [P, TILES, S], U8), sb("mask2", [P, TILES, S])
        self.mask0, self.blocks = sb("mask0", [P, P]), sb("blocks", [P, P])
        self.ident, self.ones = sb("ident", [P, P]), sb("ones", [P, P])
        self.consts, self.small = sb("consts", [P, 16]), sb("small", [P, 16])
        c = lambda i: self.consts[:, i:i + 1]
        self.c_mhalf, self.c_half, self.c_cw, self.c_icw, self.c_eps, self.c_scale = (c(i) for i in range(6))
        for_all = lambda name, n: sb(name, [P, n])
        self.w_ss, self.w_tot, self.w_scale = for_all("w_ss", 2), for_all("w_tot", 2), for_all("w_scale", 2)
        self.inv = [for_all(f"inv_{w}", 2) for w in "qkvo"]
        self.qk, self.osc, self.eps_q, self.eps_k = (for_all(n, 2) for n in ("qk", "osc", "eps_q", "eps_k"))
        self.s_c, self.inv_c, self.joint = for_all("s_c", 1), for_all("inv_c", 1), for_all("joint", 2)
        self.wqk, self.kscale, self.peak = for_all("wqk", 1), for_all("kscale", 1), for_all("peak", 8)
        self.tmp_t, self.rows = for_all("tmp", 1), for_all("rows", 8)
        self.tmp = self.tmp_t[:, 0:1]
        self.qtot, self.qtot2, self.rq = for_all("qtot", 16), for_all("qtot2", 16), sb("rq", [P, 2, 16])
        self.nmax, self.nmax2, self.rsum, self.rinv = (sb(n, [P, 2, HG]) for n in ("nmax", "nmax2", "rsum", "rinv"))
        self.bn, self.mv = sb("bn", [P, TILES, 6]), sb("mv", [P, TILES, 2])
        self.var, self.rstd = for_all("var", 8), for_all("rstd", 8)
        self.bank = [ctx.enter_context(nc.psum_tensor(f"bank{i}", [P, 512], FP32)) for i in range(8)]

    def signals(self, block, names, totals):
        out = {}
        for n in names:
            if n not in totals:
                out[n] = Signal(self.ctx.enter_context(self.nc.semaphore(f"{block}_{n}")))
                continue
            if n not in self.shared:
                self.shared[n] = Signal(self.ctx.enter_context(self.nc.semaphore(n)))
            shared = self.shared[n]
            out[n] = Signal(shared.sem, shared.base)
            shared.base += totals[n]
        return out

    def view(self, lo, shape):
        n = math.prod(shape)
        v = self.arena[:, lo:lo + n]
        if len(shape) == 2:
            return v.rearrange("p (a b) -> p a b", a=shape[0])
        if len(shape) == 3:
            return v.rearrange("p (a b c) -> p a b c", a=shape[0], b=shape[1])
        return v

    def dest(self, name, part, i):
        t = {"Q": self.Q, "K": self.K, "V": self.V}[name[0]]
        return t[:, i, part, int(name[1]), :]

    def hid_ctx(self, i, c):
        return self.hid[:, i, c, :, 0:S]

    def hid_lat(self, i, t):
        return self.hid[:, i, :, 2 * t:2 * t + 2, S:2 * S]

    def ctx_in_view(self, c):
        return self.ctx_in[:, c, :].rearrange("p (b n) -> p b n", b=B)

    def kv3(self, m, i):
        if m < 16:
            return self.kt3[:, i, m // 4, (m % 4) * 4:(m % 4) * 4 + 4, :].rearrange("p b n -> p (b n)")
        return self.v3[:, i, m - 16, :, :].rearrange("p g n -> p (g n)")

    def ln_stats(self, dve, ch, s):
        for t in range(TILES):
            ins = dve.bn_stats(self.bn[:, t, :], self.x[:, t, :])
        ins.then_inc(ch.sem, 1)
        dve.wait_ge(*ch.next())
        for t in range(TILES):
            ins = dve.bn_aggr(self.mv[:, t, :], self.bn[:, t, :])
        ins.then_inc(ch.sem, 1)
        dve.wait_ge(*ch.next())
        dve.tensor_scalar(self.var[:, :], self.mv[:, :, 1:2].rearrange("p t o -> p (t o)"), EPS, None, ALU.add)\
           .then_inc(s["stat"].sem, 1)

    def softmax8(self, dve, ch, s, lg, f):
        z3 = f.z[:, 0:64].rearrange("p (t e) -> p t e", e=E8)
        e3 = f.e[:, 0:64].rearrange("p (t e) -> p t e", e=E8)
        dve.wait_ge(*s["lg"].by(1))
        dve.tensor_reduce(f.nm[:, :], lg, AX.X, ALU.max, negate=True).then_inc(ch.sem, 1)
        dve.wait_ge(*ch.next())
        dve.tensor_tensor(z3, lg, bc(f.nm[:, :], E8), ALU.add).then_inc(s["top"].sem, 1)
        dve.wait_ge(*s["ex"].by(1))
        dve.tensor_reduce(f.nm[:, :], e3, AX.X, ALU.add).then_inc(ch.sem, 1)
        dve.wait_ge(*ch.next())
        dve.reciprocal(f.sm[:, :], f.nm[:, :]).then_inc(ch.sem, 1)
        dve.wait_ge(*ch.next())


def build(nc, d, out):
    with ExitStack() as ctx:
        k = Kernel(nc, ctx)
        setup = Setup(k, d["setup"])
        a0 = Attention(k, 0, d["a0"], setup.s["done"], 1)
        f0 = BinaryFFN(k, a0.s["xadd"], UNITS, d["f0"])
        x1 = NarrowAttention(k, f0.s["x"], TILES, d["x1"])
        f1 = FourierFFN(k, x1.s["x"], TILES, d["f1"])
        a2 = Attention(k, 2, d["a2"], f1.s["x"], TILES)
        f2 = AdapterFFN(k, 2, a2.s["xadd"], UNITS, d["f2"])
        a3 = Attention(k, 3, d["a3"], f2.s["x"], TILES)
        d["f3"]["out"] = out
        f1.follower, f2.follower = a2, a3
        f3 = AdapterFFN(k, 3, a3.s["xadd"], UNITS, d["f3"])
        blocks = [setup, a0, f0, x1, f1, a2, f2, a3, f3]
        block = ctx.enter_context(nc.Block())

        @block.sync
        def _(sp):
            for b in blocks:
                b.sp(sp)

        @block.scalar
        def _(act):
            for b in blocks:
                b.act(act)

        @block.vector
        def _(dve):
            for b in blocks:
                b.dve(dve)

        @block.tensor
        def _(pe):
            for b in blocks[1:]:
                b.pe(pe)

        @block.gpsimd
        def _(pool):
            for b in blocks:
                b.pool(pool)


def fourier(n):
    import numpy as np
    j = np.arange(n)
    f = np.zeros((n, n))
    f[0] = 1.0 / math.sqrt(n)
    f[n - 1] = np.cos(np.pi * j) / math.sqrt(n)
    for q in range(1, n // 2):
        f[2 * q - 1] = math.sqrt(2.0 / n) * np.cos(2 * np.pi * ((q * j) % n) / n)
        f[2 * q] = math.sqrt(2.0 / n) * np.sin(2 * np.pi * ((q * j) % n) / n)
    return f.astype(np.float32)


def kernel(**inputs):
    import numpy as np
    import concourse.bacc as _bacc
    from concourse.bass_utils import run_bass_kernel_spmd as _run

    nc = _bacc.Bacc("TRN2", target_bir_lowering=False, num_devices=1)
    i = {n: np.asarray(a) for n, a in inputs.items()}
    arrays = {}

    def dram(name, a):
        a = np.ascontiguousarray(a)
        arrays[name] = a
        return nc.dram_tensor(name, a.shape, mybir.dt.from_np(a.dtype), kind="ExternalInput").ap()

    def chunks(w):
        return w.reshape(-1, P, w.shape[-1]).transpose(1, 0, 2)

    def slabs(w, n):
        g = w.shape[1] // n
        return w.reshape(KC, P, g, n).transpose(2, 1, 0, 3).reshape(g, P, KC * n)

    def rows(w):
        g = w.shape[0] // 512
        return w.reshape(g, 4, P, D).transpose(0, 2, 1, 3).reshape(g, P, 4 * D)

    ctx = i["ctx_4096"].reshape(TOK, D)
    ctx_nat, ctx_t = dram("ctx", chunks(ctx)), dram("ctx_t", chunks(ctx.T))
    d = {
        "setup": {"x": dram("x", chunks(i["x"].reshape(TOK, D))), "ctx": ctx_nat, "ctx_t": ctx_t,
                  "qn": dram("qn", i["L0_xattn_q_norm_w"].reshape(P, 1)),
                  "kn": dram("kn", i["L0_xattn_k_norm_w"].reshape(P, 1)),
                  "mask": dram("mask0_in", i["mask_1x1xSxS2_ff0"].reshape(S, S))},
        "a0": {"q": dram("a0_q", slabs(i["L0_xattn_q_proj_w"].T, 512)),
               "k": dram("a0_k", slabs(i["L0_xattn_k_proj_w"].T, P)),
               "v": dram("a0_v", slabs(i["L0_xattn_v_proj_w"].T, P)),
               "o": dram("a0_o", rows(i["L0_xattn_o_proj_w"].T))},
        "f0": {"w": dram("f0_w", chunks(i["L0_ffn_weight"].T)), "gate": dram("f0_gate", chunks(i["L0_ffn_gate_w"].T)),
               "ics": dram("f0_ics", i["L0_ffn_in_channel_scale"]), "ocs": dram("f0_ocs", i["L0_ffn_out_channel_scale"]),
               "bias": dram("f0_b", i["L0_ffn_bias"])},
        "x1": {"ctx": ctx_nat, "ctx_t": ctx_t, "wq": dram("x1_q", chunks(i["L1_xattn_Wq"].T)),
               "wk": dram("x1_k", chunks(i["L1_xattn_Wk"].T)),
               "bq": dram("x1_bq", i["L1_xattn_bq"].reshape(KC, P).T),
               "bk": dram("x1_bk", i["L1_xattn_bk"].reshape(KC, P).T)},
        "a2": {"q": dram("a2_q", slabs(i["L2_xattn_Wq"], 512)), "k": dram("a2_k", slabs(i["L2_xattn_Wk"], 512)),
               "v": dram("a2_v", slabs(i["L2_xattn_Wv"], 512)), "o": dram("a2_o", rows(i["L2_xattn_Wo"])),
               "mask": dram("mask2_in", i["mask_BxSxS2_bk0"].reshape(TILES, P, S).transpose(1, 0, 2)),
               "bias": dram("bias2", i["fside_Bx32xSxS2_0"].reshape(TILES, 2, GROUPS, HG, S, S)
                            .transpose(2, 0, 1, 4, 3, 5).reshape(UNITS, P, HG * S))},
        "a3": {"q": dram("a3_q", slabs(i["L3_xattn_Wq"], 512)), "k": dram("a3_k", slabs(i["L3_xattn_Wk"], 512)),
               "v": dram("a3_v", slabs(i["L3_xattn_Wv"], 512)), "o": dram("a3_o", rows(i["L3_xattn_Wo"])),
               "ctx_t": ctx_t},
    }
    co = np.concatenate([i["L1_ffn_coefs0"], i["L1_ffn_coefs1"]], axis=2)
    mk = np.concatenate([i["L1_ffn_mask0"], i["L1_ffn_mask1"]], axis=2)
    by_row = lambda w: w.reshape(3, KC, P, R40).transpose(2, 1, 0, 3)
    d["f1"] = {"co": dram("f1_co", by_row(co)), "mask": dram("f1_mask", by_row(mk)),
               "f": dram("f1_fourier", chunks(fourier(D))),
               "enc": dram("f1_enc", chunks(np.concatenate([i["L1_ffn_enc0"], i["L1_ffn_enc1"]]).T)),
               "w": dram("f1_w", chunks(i["L1_ffn_W_base"].T)), "bias": dram("f1_b", i["L1_ffn_b_base"].reshape(1, D))}
    d["f2"] = {"w": dram("f2_w", chunks(i["L2_ffn_W_base"].T)),
               "gate": dram("f2_gate", chunks(np.concatenate([i["L2_ffn_W_gate"], i["L2_ffn_W_thr"][None]]).T)),
               "a": dram("f2_a", chunks(i["L2_ffn_A_w"].reshape(P, D).T)),
               "bm": dram("f2_bm", i["L2_ffn_B_w"].transpose(0, 2, 1).reshape(P, D)),
               "bias": dram("f2_b", i["L2_ffn_b_base"]), "bthr": dram("f2_bt", i["L2_ffn_b_thr"])}
    d["f3"] = {"w": dram("f3_w", chunks(i["L3_ffn_W_base"].T)), "gate": dram("f3_gate", chunks(i["L3_ffn_W_router"].T)),
               "a": dram("f3_a", chunks(i["L3_ffn_A"].reshape(P, D).T)),
               "bm": dram("f3_bm", i["L3_ffn_B"].transpose(0, 2, 1).reshape(P, D)),
               "bias": dram("f3_b", i["L3_ffn_b_base"])}
    out = nc.dram_tensor("out", (TOK, D), FP32, kind="ExternalOutput").ap()
    build(nc, d, out)
    r = _run(nc, [arrays], core_ids=[0])
    return r.results[0]["out"].reshape(B, S, D)
```
